# Optimizing a Trainium2 kernel written in Bass

```python
import numpy as np
import jax
import jax.numpy as jnp

def _softmax(x, axis=-1):
    return jax.nn.softmax(x, axis=axis)

def _gelu(x):
    return jax.nn.gelu(x, approximate=True)

def _silu(x):
    return jax.nn.silu(x)

def _sigmoid(x):
    return jax.nn.sigmoid(x)

def _layernorm(x, axis=-1, eps=1e-05):
    m = jnp.mean(x, axis=axis, keepdims=True)
    v = jnp.var(x, axis=axis, keepdims=True)
    return (x - m) / jnp.sqrt(v + eps)

def _scatter_add(tgt, idx, src, axis=0):
    return tgt.at[idx].add(src)

def _segment_sum(src, seg, n):
    return jax.ops.segment_sum(src, seg, n)
kernel_name = 'mk_adj_resnorm_d2_adj_r2_051084'

def setup_inputs(seed: int=0):
    np.random.seed(seed)
    _w = jnp.asarray

    def _rec_inputs():
        import jax
        import jax.numpy as jnp
        _gk = jax.random.key(seed)
        x = 7.22e-05 + 1 * jax.random.normal(jax.random.fold_in(_gk, 1), (128, 128, 512), jnp.float32)
        _w = (1.0 + jnp.arange(128, dtype=jnp.float32)) ** (-0.5)
        _w = _w / _w.mean()
        _pij = jnp.clip(0.125 * _w[:, None] * _w[None, :], 0.0, 1.0)
        _a = jax.random.uniform(jax.random.fold_in(_gk, 2), (128, 128, 128)) < _pij
        _a = jnp.logical_or(_a, jnp.swapaxes(_a, -1, -2))
        _a = jnp.logical_or(_a, jnp.eye(128, dtype=bool))
        _af = _a.astype(jnp.float32)
        _af = _af * jax.random.uniform(jax.random.fold_in(_gk, 3), (128, 128, 128), jnp.float32, 0.05, 4.42607)
        adj = _af
        return (x, adj)
    x, adj = _rec_inputs()

    def _L0_gnn_setup():
        import jax, jax.numpy as jnp
        import numpy as np
        NUM_HEADS = 16
        key = jax.random.key(seed)
        ks = jax.random.split(key, 7)
        B, N, D = (16, 256, 512)
        return {'x': jax.random.normal(ks[0], (B, N, D), dtype=jnp.float32), 'spatial_encoding': jax.random.normal(ks[1], (B, N, N), dtype=jnp.float32), 'edge_encoding': jax.random.normal(ks[2], (B, N, N), dtype=jnp.float32), 'Wq': jax.random.normal(ks[3], (D, D), dtype=jnp.float32) * D ** (-0.5), 'Wk': jax.random.normal(ks[4], (D, D), dtype=jnp.float32) * D ** (-0.5), 'Wv': jax.random.normal(ks[5], (D, D), dtype=jnp.float32) * D ** (-0.5), 'Wo': jax.random.normal(ks[6], (D, D), dtype=jnp.float32) * D ** (-0.5)}
    _L0_gnn_all = _L0_gnn_setup()
    _L0_gnn_in = {k: v for k, v in _L0_gnn_all.items() if k in ('Wq', 'Wk', 'Wv', 'Wo')}
    del _L0_gnn_all

    def _L1_gnn_setup():
        import jax, jax.numpy as jnp
        import numpy as np
        B, N, H, E = (64, 256, 512, 4)
        BN_EPS = 1e-05
        key = jax.random.key(seed)
        ks = jax.random.split(key, 6)
        x = jax.random.normal(ks[0], (B, N, H), dtype=jnp.float32)
        adj = jax.random.uniform(ks[1], (B, N, N), dtype=jnp.float32)
        stdv = 1.0 / np.sqrt(H)
        expert_w = jax.random.uniform(ks[2], (E, H, H), minval=-stdv, maxval=stdv, dtype=jnp.float32)
        r_std = 1.0 / np.sqrt(H)
        router_w = jax.random.uniform(ks[3], (H, E), minval=-r_std, maxval=r_std, dtype=jnp.float32)
        router_b = jax.random.uniform(ks[4], (E,), minval=-r_std, maxval=r_std, dtype=jnp.float32)
        bn_gamma = jnp.ones((E, H), dtype=jnp.float32)
        bn_beta = jnp.zeros((E, H), dtype=jnp.float32)
        return {'x': x, 'adj': adj, 'router_w': router_w, 'router_b': router_b, 'expert_w': expert_w, 'bn_gamma': bn_gamma, 'bn_beta': bn_beta}
    _L1_gnn_all = _L1_gnn_setup()
    _L1_gnn_in = {k: v for k, v in _L1_gnn_all.items() if k in ('router_w', 'router_b', 'expert_w', 'bn_gamma', 'bn_beta')}
    del _L1_gnn_all
    return {'x': x, 'adj': adj, 'L0_gnn_Wq': _L0_gnn_in['Wq'], 'L0_gnn_Wk': _L0_gnn_in['Wk'], 'L0_gnn_Wv': _L0_gnn_in['Wv'], 'L0_gnn_Wo': _L0_gnn_in['Wo'], 'L1_gnn_router_w': _L1_gnn_in['router_w'], 'L1_gnn_router_b': _L1_gnn_in['router_b'], 'L1_gnn_expert_w': _L1_gnn_in['expert_w'], 'L1_gnn_bn_gamma': _L1_gnn_in['bn_gamma'], 'L1_gnn_bn_beta': _L1_gnn_in['bn_beta']}

def reference(x, adj, L0_gnn_Wq, L0_gnn_Wk, L0_gnn_Wv, L0_gnn_Wo, L1_gnn_router_w, L1_gnn_router_b, L1_gnn_expert_w, L1_gnn_bn_gamma, L1_gnn_bn_beta):
    import jax
    import jax.numpy as jnp

    def _L0_gnn_ref(x, spatial_encoding, edge_encoding, Wq, Wk, Wv, Wo):
        import jax, jax.numpy as jnp
        import numpy as np
        NUM_HEADS = 16
        B, N, D = x.shape
        H = NUM_HEADS
        hd = D // H
        scale = D ** (-0.5)

        def split_heads(t):
            return t.reshape(B, N, H, hd).transpose(0, 2, 1, 3)
        q = split_heads(x @ Wq.T)
        k = split_heads(x @ Wk.T)
        v = split_heads(x @ Wv.T)
        bias = (spatial_encoding + edge_encoding)[:, None]
        a = jnp.einsum('bhnd,bhmd->bhnm', q, k) * scale + bias
        row_nonzero = jnp.any(a != 0, axis=-1, keepdims=True)
        a = jnp.where(row_nonzero, a, -jnp.inf)
        p = jax.nn.softmax(a, axis=-1)
        p = jnp.where(jnp.isnan(p), 0.0, p)
        o = jnp.einsum('bhnm,bhmd->bhnd', p, v)
        o = o.transpose(0, 2, 1, 3).reshape(B, N, D)
        return o @ Wo.T

    def _L1_gnn_ref(x, adj, router_w, router_b, expert_w, bn_gamma, bn_beta):
        import jax, jax.numpy as jnp
        import numpy as np
        B, N, H, E = (64, 256, 512, 4)
        BN_EPS = 1e-05
        scores = x.mean(axis=1) @ router_w + router_b
        top1 = jnp.argmax(scores, axis=-1)
        n_exp = expert_w.shape[0]
        W = expert_w[top1]
        support = jnp.einsum('bnh,bhk->bnk', x, W)
        out = jnp.einsum('bnm,bmk->bnk', adj, support)
        s = jax.ops.segment_sum(out.sum(axis=1), top1, num_segments=n_exp)
        ss = jax.ops.segment_sum((out * out).sum(axis=1), top1, num_segments=n_exp)
        cnt = jax.ops.segment_sum(jnp.ones_like(top1, dtype=out.dtype), top1, num_segments=n_exp) * out.shape[1]
        cnt = jnp.maximum(cnt, 1.0)[:, None]
        mean = s / cnt
        var = ss / cnt - mean * mean
        m = mean[top1][:, None, :]
        inv = jax.lax.rsqrt(var[top1][:, None, :] + BN_EPS)
        y = (out - m) * inv * bn_gamma[top1][:, None, :] + bn_beta[top1][:, None, :]
        return jax.nn.relu(y)
    x = _layernorm(x + _L0_gnn_ref(x, adj, adj, L0_gnn_Wq, L0_gnn_Wk, L0_gnn_Wv, L0_gnn_Wo), axis=-1)
    x = _layernorm(x + _L1_gnn_ref(x, adj, L1_gnn_router_w, L1_gnn_router_b, L1_gnn_expert_w, L1_gnn_bn_gamma, L1_gnn_bn_beta), axis=-1)
    return x

_drawn_inputs = setup_inputs


def setup_inputs(seed=0):
    import zlib

    import numpy as np

    out = dict(_drawn_inputs(seed))
    spreads = {'L1_gnn_bn_gamma': (1.0, 0.2), 'L1_gnn_bn_beta': (0.0, 0.1)}
    factors = {}
    for name, (base, spread) in spreads.items():
        noise = np.random.default_rng([zlib.crc32(name.encode()), seed]).standard_normal(out[name].shape)
        drawn = base * np.exp(spread * noise) if base else spread * noise
        out[name] = jnp.asarray(drawn.astype(out[name].dtype))
    for name, factor in factors.items():
        out[name] = (out[name] * factor).astype(out[name].dtype)
    return out
```

```python
from contextlib import ExitStack

import concourse.bass as bass
from concourse import mybir
from concourse.alu_op_type import AluOpType as ALU

F32 = mybir.dt.float32
F32R = mybir.dt.float32r
I32 = mybir.dt.int32
ACT = mybir.ActivationFunctionType
AX = mybir.AxisListType

P = 128
HEADS = 16
EPS = 1e-5


def graph_block_program(nc, x, xT, adj, adjT, wqT, wkT, wvT, woT, router_w, router_b, expert_w,
                        gamma, beta, out):
    B, N, D = x.shape
    E = router_w.shape[2]
    C = D // P
    HPC = HEADS // C
    HD = D // HEADS
    HALF_SCALE = 0.5 * float(D) ** -0.5
    assert N == P and HD == 32 and B % 4 == 0 and B >= 20

    x1_dram = nc.dram_tensor("x1_scratch", (P, B, D), F32, kind="Internal").ap()
    conv_dram = nc.dram_tensor("conv_scratch", (P, B, D), F32, kind="Internal").ap()

    with ExitStack() as ctx:
        def sem(name):
            return ctx.enter_context(nc.semaphore(name))

        expert_of = ctx.enter_context(nc.sbuf_tensor("expert_of", [P, B], I32))
        square_sum = ctx.enter_context(nc.sbuf_tensor("square_sum", [P, E * D], F32))
        conv_sum = ctx.enter_context(nc.sbuf_tensor("conv_sum", [P, E, C], F32))
        count = ctx.enter_context(nc.sbuf_tensor("count", [P, E], F32))
        experts = ctx.enter_context(nc.sbuf_tensor("experts", [P, E * C * D], F32))
        minus_half = ctx.enter_context(nc.sbuf_tensor("minus_half", [P, 1], F32))
        ones = ctx.enter_context(nc.sbuf_tensor("ones", [P, P], F32))
        bank = [ctx.enter_context(nc.psum_tensor(f"bank{i}", [P, 512], F32)) for i in range(8)]
        ps_scores, ps_turned = bank[0:2], bank[2:4]
        ps_a, ps_b, ps_c, ps_small = bank[4:8]

        p1 = ExitStack()

        def sb(name, shape, dt=F32):
            return p1.enter_context(nc.sbuf_tensor(name, shape, dt))

        w_hi = {k: sb(f"w{k}_hi", [P, C, D], F32R) for k in "qkvo"}
        w_lo = {k: sb(f"w{k}_lo", [P, C, D], F32R) for k in "qkvo"}
        xT_in = sb("xT_in", [P, C, 2 * P])
        xT_hi = sb("xT_hi", [P, 2, C, 2 * P], F32R)
        xT_lo = sb("xT_lo", [P, 2, C, 2 * P], F32R)
        x_in = sb("x_in", [P, 2, D])
        adj_in = sb("adj_in", [P, 2, 2, P])
        adjT_in = sb("adjT_in", [P, 2, 2, P])
        qk = sb("qk", [P, 2, C, 2, 2 * P])
        v = sb("v", [P, 4, D])
        k_diag = sb("k_diag", [P, C, HPC, P])
        prob = sb("prob", [P, 2, HEADS, P])
        probT = sb("probT", [P, HEADS, P])
        oT_hi = sb("oT_hi", [P, C, P], F32R)
        oT_lo = sb("oT_lo", [P, C, P], F32R)
        x1 = sb("x1", [P, 2, D])
        yT = sb("yT", [P, C, P])
        conv = sb("conv", [P, 2, D])
        square = sb("square", [P, D])
        ident = sb("ident", [P, P])
        head_rows = sb("head_rows", [P, HPC])
        rw = sb("rw", [P, C, E])
        rb = sb("rb", [P, E])
        neg_max = sb("neg_max", [P, 2, HEADS])
        neg_max2 = sb("neg_max2", [P, 2, HEADS])
        abs_max = sb("abs_max", [P, 2, HEADS])
        row_sum = sb("row_sum", [P, 2, HEADS])
        inv_sum = sb("inv_sum", [P, HEADS])
        inv_nz = sb("inv_nz", [P, HEADS])
        stats = sb("stats", [P, 6])
        mean_var = sb("mean_var", [P, 2])
        var_eps = sb("var_eps", [P, 1])
        rstd = sb("rstd", [P, 1])
        row_and_mean = sb("row_and_mean", [P, 2, 2])
        sums = sb("sums", [P, C, 2])
        logits = sb("logits", [P, E])
        top = sb("top", [P, 1])
        rank = sb("rank", [P, E])
        ranked = sb("ranked", [P, E])
        best = sb("best", [P, 1])
        neg_best = sb("neg_best", [P, 1])
        one_hot = sb("one_hot", [P, E])
        picked = sb("picked", [P, E, C])

        ld_w = [sem(f"ld_w{i}") for i in range(4)]
        ld_const = sem("ld_const")
        ld_xT = sem("ld_xT")
        ld_x = [sem("ld_x0"), sem("ld_x1")]
        ld_adj = [sem("ld_adj0"), sem("ld_adj1")]
        ld_adjT = [sem("ld_adjT0"), sem("ld_adjT1")]
        st_x1 = [sem("st_x1_0"), sem("st_x1_1")]
        st_conv = [sem("st_conv0"), sem("st_conv1")]
        pool_zeroed = sem("pool_zeroed")
        pool_ready = sem("pool_ready")
        pool_passed = sem("pool_passed")
        x_split = sem("x_split")
        x_rounded = sem("x_rounded")
        diag_built = sem("diag_built")
        squares_added = sem("squares_added")
        rstd_made = sem("rstd_made")
        scores_done = sem("scores_done")
        qk_done = sem("qk_done")
        v_done = sem("v_done")
        turned = sem("turned")
        pv_done = sem("pv_done")
        proj_done = sem("proj_done")
        y_done = sem("y_done")
        router_done = sem("router_done")
        conv_done = sem("conv_done")
        qk_copied = sem("qk_copied")
        v_copied = sem("v_copied")
        probT_copied = sem("probT_copied")
        exp_done = sem("exp_done")
        oT_rounded = sem("oT_rounded")
        y_copied = sem("y_copied")
        conv_copied = sem("conv_copied")
        squared = sem("squared")
        w_rounded = sem("w_rounded")
        w_split = sem("w_split")
        rows_cleared = sem("rows_cleared")
        consts_set = sem("consts_set")
        biased = sem("biased")
        max_found = sem("max_found")
        max_doubled = sem("max_doubled")
        abs_found = sem("abs_found")
        sum_inverted = sem("sum_inverted")
        zero_rows_out = sem("zero_rows_out")
        normalised = sem("normalised")
        oT_split = sem("oT_split")
        residual_added = sem("residual_added")
        stats_taken = sem("stats_taken")
        stats_joined = sem("stats_joined")
        var_ready = sem("var_ready")
        x1_ready = sem("x1_ready")
        rows_summed = sem("rows_summed")
        sums_copied = sem("sums_copied")
        logits_made = sem("logits_made")
        top_found = sem("top_found")
        ranked_made = sem("ranked_made")
        best_found = sem("best_found")
        best_negated = sem("best_negated")
        hot_made = sem("hot_made")
        expert_known = sem("expert_known")
        picked_made = sem("picked_made")
        stats_added = sem("stats_added")

        SLOT_LOOP_START, SLOT_LOOP_END, SLOT_END = 8, B - 8, B + 5

        def run_slots(eng, slot, first):
            for t in range(first, SLOT_LOOP_START):
                slot(t // 4, t % 4, lambda b: 0 <= b < B)
            with eng.Fori(SLOT_LOOP_START // 4, SLOT_LOOP_END // 4, 1) as i:
                for u in range(4):
                    slot(i, u, lambda b: True)
            for t in range(SLOT_LOOP_END, SLOT_END):
                slot(t // 4, t % 4, lambda b: 0 <= b < B)

        def wait(eng, s, value):
            if not isinstance(value, int) or value > 0:
                eng.wait_ge(s, value)

        def half(i, u, k=0):
            return i * 2 + (u + k) // 2

        def quarter(i, u, k=0):
            return i + (u + k) // 4

        def pv_mod(u, k, m):
            return (u + k) % m

        READY = 7 + E

        phase_one = ExitStack()
        block = phase_one.enter_context(nc.Block())

        @block.sync
        def _(sp):
            def load_xT(pair):
                wait(sp, x_split, pair)
                sp.dma_start(xT_in[:, :, :], xT[:, bass.ds(pair, 1), :].rearrange(
                    "p g (c n) -> p (g c) n", c=C)).then_inc(ld_xT, 16)

            for i, (k, w) in enumerate(zip("vqko", (wvT, wqT, wkT, woT))):
                if i == 1:
                    load_xT(0)
                if i >= 2:
                    sp.wait_ge(w_split, i - 1)
                sp.dma_start(prob[:, i % 2, :, :].rearrange("p h m -> p (h m)"),
                             w).then_inc(ld_w[i], 16)
            for dst, src in ((rw[:, :, :], router_w), (rb[:, :], router_b.partition_broadcast(P)),
                             (experts[:, :], expert_w)):
                sp.dma_start(dst, src).then_inc(ld_const, 16)

            def slot(i, u, live):
                t = i * 4 + u
                b = t - 3
                if live(b):
                    wait(sp, x1_ready, b + 1)
                    par = pv_mod(u, -3, 2)
                    sp.dma_start(x1_dram[:, bass.ds(b, 1), :].rearrange("p b d -> p (b d)"),
                                 x1[:, par, :]).then_inc(st_x1[par], 16)
                b = t - 5
                if live(b):
                    wait(sp, conv_copied, b + 1)
                    par = pv_mod(u, -5, 2)
                    sp.dma_start(conv_dram[:, bass.ds(b, 1), :].rearrange("p b d -> p (b d)"),
                                 conv[:, par, :]).then_inc(st_conv[par], 16)
                if live(t):
                    wait(sp, residual_added, t - 1)
                    sp.dma_start(x_in[:, u % 2, :], x[bass.ds(t, 1), :, :].rearrange(
                        "b n d -> n (b d)")).then_inc(ld_x[u % 2], 16)
                if u % 2 == 0:
                    g = half(i, u)
                    pair = g + 1
                    if live(2 * pair):
                        par = (u // 2 + 1) % 2
                        wait(sp, biased, 8 * g)
                        sp.dma_start(adj_in[:, par, :, :], adj[bass.ds(2 * pair, 2), :, :].rearrange(
                            "b n m -> n b m")).then_inc(ld_adj[par], 16)
                    pair = g - 1
                    if live(2 * pair):
                        par = (u // 2 + 1) % 2
                        wait(sp, y_done, 2 * g - 4)
                        sp.dma_start(adjT_in[:, par, :, :], adjT[:, bass.ds(2 * pair, 2), :]
                                     ).then_inc(ld_adjT[par], 16)
                    if live(2 * (g + 3)) and (not isinstance(t, int) or g + 3 > 0):
                        load_xT(g + 3)

            run_slots(sp, slot, -4)
            for par in range(2):
                sp.wait_ge(st_x1[par], 16 * (B // 2))
                sp.wait_ge(st_conv[par], 16 * (B // 2))

        @block.gpsimd
        def _(pool):
            pool.memset(ident[:, :], 0.0).then_inc(pool_zeroed, 1)
            pool.memset(square_sum[:, :], 0.0).then_inc(pool_ready, 1)
            pool.memset(conv_sum[:, :, :], 0.0).then_inc(pool_ready, 1)
            pool.memset(count[:, :], 0.0).then_inc(pool_ready, 1)
            pool.memset(row_and_mean[:, :, 1:2], 1.0 / N).then_inc(pool_ready, 1)
            pool.memset(ones[:, :], 1.0).then_inc(pool_ready, 1)
            pool.memset(minus_half[:, :], -0.5).then_inc(pool_ready, 1)
            for e in range(E):
                pool.memset(rank[:, e:e + 1], float(E - e)).then_inc(pool_ready, 1)
            pool.wait_ge(pool_zeroed, 1)
            pool.affine_select(out=ident[:, :], in_=ident[:, :], compare_op=ALU.not_equal, fill=1.0,
                               base=0, pattern=[[-1, P]], channel_multiplier=1).then_inc(pool_ready, 1)
            pool.wait_ge(pool_ready, READY - 1)

            pool.wait_ge(consts_set, HPC)

            def split_xT(pair, par):
                wait(pool, ld_xT, 16 * (pair + 1))
                wait(pool, v_done, 2 * pair - 2)
                wait(pool, qk_done, C * (pair - 1))
                pool.sem_inc(pool_passed)
                pool.tensor_copy(xT_hi[:, par, :, :], xT_in[:, :, :]).then_inc(x_rounded, 1)
                wait(pool, x_rounded, pair + 1)
                pool.tensor_tensor(xT_lo[:, par, :, :], xT_in[:, :, :],
                                   xT_hi[:, par, :, :].bitcast(F32), ALU.subtract).then_inc(x_split, 1)

            def slot(i, u, live):
                t = i * 4 + u
                b = t + 1
                if live(b):
                    pair, side = half(i, u, 1), (u + 1) % 2
                    par = pv_mod(u, 1, 4) // 2
                    wait(pool, qk_copied, C * (pair + 1))
                    wait(pool, scores_done, C * b)
                    pool.sem_inc(pool_passed)
                    for h in range(HPC):
                        last = pool.tensor_scalar(k_diag[:, :, h, :], qk[:, par, :, 1, side * P:side * P + P],
                                                  head_rows[:, h:h + 1], None, ALU.mult)
                    last.then_inc(diag_built, 1)
                if u % 2 == 0:
                    pair = half(i, u) + 2
                    if live(2 * pair):
                        split_xT(pair, (u // 2) % 2)
                if live(t - 2):
                    wait(pool, var_ready, t - 1)
                    pool.tensor_tensor(rstd[:, :], var_eps[:, :], minus_half[:, 0:1],
                                       ALU.pow).then_inc(rstd_made, 1)
                b = t - 4
                if live(b):
                    wait(pool, expert_known, b + 1)
                    e = pool.value_load(expert_of[0:1, bass.ds(b, 1)], min_val=0, max_val=E - 1)
                    wait(pool, squared, b + 1)
                    wait(pool, squares_added, b)
                    acc = square_sum[:, bass.ds(e * D, D)]
                    pool.tensor_tensor(acc, acc, square[:, :], ALU.add).then_inc(squares_added, 1)

            run_slots(pool, slot, -4)

        @block.tensor
        def _(pe):
            def mm(dst, lhsT, rhs, start, stop):
                return pe.matmul(dst, lhsT, rhs, start=start, stop=stop)

            def mm3(dst, lhs, rhs):
                n = len(lhs)
                for i, ((lh, ll), (rh, rl)) in enumerate(zip(lhs, rhs)):
                    mm(dst, lh, rh, i == 0, False)
                    mm(dst, lh, rl, False, False)
                    last = mm(dst, ll, rh, False, i == n - 1)
                return last

            pe.wait_ge(pool_ready, READY)
            pe.wait_ge(w_split, 4)
            pe.wait_ge(ld_const, 48)

            def slot(i, u, live):
                t = i * 4 + u
                pair = half(i, u)
                par = u // 2

                def scores(c):
                    b = t
                    if not live(b):
                        return
                    if c == 0:
                        wait(pe, qk_copied, C * (pair + 1))
                        wait(pe, diag_built, b + 1)
                    wait(pe, biased, C * b + c - 1)
                    side = u % 2
                    mm(ps_scores[c % 2][:, :], qk[:, par, c, 0, side * P:side * P + P],
                       k_diag[:, c, :, :].rearrange("p h m -> p (h m)"), True, True
                       ).then_inc(scores_done, 1)

                def project_qk(c, dst):
                    nxt, npar = pair + 1, (par + 1) % 2
                    if not live(2 * nxt):
                        return
                    wait(pe, x_split, nxt + 1)
                    for i, k in enumerate("qk"):
                        last = mm3(dst[:, i * 2 * P:(i + 1) * 2 * P],
                                   [(w_hi[k][:, j, c * P:(c + 1) * P], w_lo[k][:, j, c * P:(c + 1) * P])
                                    for j in range(C)],
                                   [(xT_hi[:, npar, j, :], xT_lo[:, npar, j, :]) for j in range(C)])
                    last.then_inc(qk_done, 1)

                def turn(c):
                    b = t - 1
                    if not live(b):
                        return
                    if c == 0:
                        wait(pe, normalised, b + 1)
                    wait(pe, probT_copied, C * b + c - 1)
                    for h in range(HPC):
                        last = pe.transpose(ps_turned[c % 2][:, h * P:(h + 1) * P],
                                            prob[:, pv_mod(u, -1, 2), HPC * c + h, :], ident[:, :])
                    last.then_inc(turned, 1)

                def times_v(c):
                    b = t - 1
                    if not live(b):
                        return
                    if c == 0:
                        wait(pe, v_copied, b + 1)
                        wait(pe, y_copied, b - 2)
                        wait(pe, sums_copied, b - 2)
                    wait(pe, probT_copied, C * b + c + 1)
                    for h in range(HPC):
                        col = (HPC * c + h) * HD
                        last = mm(ps_c[HD * h:HD * h + HD, c * P:(c + 1) * P],
                                  v[:, pv_mod(u, -1, 4), col:col + HD], probT[:, HPC * c + h, :], True, True)
                    if c == C - 1:
                        last.then_inc(pv_done, 1)

                scores(0)
                scores(1)
                b = t - 4
                if live(b):
                    wait(pe, sums_copied, b + 1)
                    for c in range(C):
                        last = mm(ps_small[:, 2 * C:2 * C + E], sums[:, c, 1:2].to_broadcast([P, P]),
                                  rw[:, c, :], c == 0, c == C - 1)
                    last.then_inc(router_done, 1)
                b5 = t - 5
                if live(2 * (pair + 1)):
                    if live(b5):
                        wait(pe, squared, b5 + 1)
                    else:
                        wait(pe, v_copied, t + 2)
                project_qk((2 * u) % C, ps_a)
                scores(2)
                scores(3)
                if live(2 * (pair + 1)):
                    if live(t - 3):
                        wait(pe, residual_added, t - 2)
                    else:
                        wait(pe, qk_copied, C * (pair + 1) + (2 * u) % C)
                project_qk((2 * u) % C + 1, ps_b)
                turn(0)
                turn(1)
                b = t + 2
                if live(b):
                    nxt, npar = pair + 1, (par + 1) % 2
                    wait(pe, qk_copied, C * nxt + (2 * u) % C + 1)
                    mm3(ps_a[:, :],
                        [(xT_hi[:, npar, j, u % 2 * P:u % 2 * P + P], xT_lo[:, npar, j, u % 2 * P:u % 2 * P + P])
                         for j in range(C)],
                        [(w_hi["v"][:, j, :], w_lo["v"][:, j, :]) for j in range(C)]).then_inc(v_done, 1)
                turn(2)
                turn(3)
                times_v(0)
                times_v(1)
                b = t - 2
                if live(b):
                    wait(pe, oT_split, b + 1)
                    if live(2 * (pair + 1)):
                        wait(pe, qk_copied, C * (pair + 1) + (2 * u) % C + 2)
                    else:
                        wait(pe, residual_added, b)
                    mm3(ps_b[:, :], [(oT_hi[:, j, :], oT_lo[:, j, :]) for j in range(C)],
                        [(w_hi["o"][:, j, :], w_lo["o"][:, j, :]) for j in range(C)]).then_inc(proj_done, 1)
                times_v(2)
                times_v(3)
                b = t - 4
                if live(b):
                    wait(pe, expert_known, b + 1)
                    e = pe.value_load(expert_of[0:1, bass.ds(b, 1)], min_val=0, max_val=E - 1)
                    wait(pe, y_copied, b + 1)
                    if live(t + 2):
                        wait(pe, v_copied, t + 3)
                    else:
                        wait(pe, squared, b)
                    for c in range(C):
                        last = mm(ps_a[:, :], yT[:, c, :], experts[:, bass.ds((e * C + c) * D, D)],
                                  c == 0, c == C - 1)
                    last.then_inc(conv_done, 1)
                b = t - 3
                if live(b):
                    p4 = pv_mod(u, -3, 4)
                    wait(pe, x1_ready, b + 1)
                    wait(pe, rows_summed, b + 1)
                    if live(t - 1):
                        wait(pe, oT_split, t)
                    else:
                        wait(pe, y_copied, b)
                    wait(pe, expert_known, b)
                    for c in range(C):
                        lhsT = x1[:, p4 % 2, c * P:(c + 1) * P]
                        mm(ps_c[:, c * P:(c + 1) * P], lhsT, adjT_in[:, p4 // 2, p4 % 2, :], True, True)
                        last = mm(ps_small[:, 2 * c:2 * c + 2], lhsT, row_and_mean[:, p4 % 2, :], True, True)
                    last.then_inc(y_done, 1)

            run_slots(pe, slot, -2)

        @block.scalar
        def _(act):
            def slot(i, u, live):
                t = i * 4 + u
                pair, par = half(i, u), u // 2
                nxt, npar = pair + 1, (par + 1) % 2
                b = t - 4
                if live(b):
                    wait(act, y_done, b + 1)
                    wait(act, conv_done, b)
                    act.activation(yT[:, :, :].rearrange("p c n -> p (c n)"), ps_c[:, :],
                                   ACT.Copy).then_inc(y_copied, 1)

                def copy_qk(c, src):
                    if live(2 * nxt):
                        wait(act, qk_done, C * nxt + c + 1)
                        wait(act, scores_done, 2 * C * (nxt - 1))
                        act.activation(qk[:, npar, c, :, :].rearrange("p k n -> p (k n)"), src[:, :],
                                       ACT.Copy).then_inc(qk_copied, 1)

                def copy_turned(c):
                    if live(t - 1):
                        wait(act, turned, C * (t - 1) + c + 1)
                        wait(act, pv_done, t - 1)
                        act.activation(probT[:, HPC * c:HPC * (c + 1), :].rearrange("p h n -> p (h n)"),
                                       ps_turned[c % 2][:, :], ACT.Copy).then_inc(probT_copied, 1)

                def exps(h0, h1):
                    if live(t):
                        wait(act, max_doubled, t + 1)
                        for h in range(h0, h1):
                            last = act.activation(prob[:, u % 2, h, :], prob[:, u % 2, h, :], ACT.Exp,
                                                  bias=neg_max2[:, u % 2, h:h + 1], scale=2.0,
                                                  accum_out=row_sum[:, u % 2, h:h + 1])
                        if h1 == HEADS:
                            last.then_inc(exp_done, 1)

                copy_qk((2 * u) % C, ps_a)
                copy_qk((2 * u) % C + 1, ps_b)
                copy_turned(0)
                copy_turned(1)
                if live(t):
                    wait(act, abs_found, t + 1)
                exps(0, HEADS // 2)
                if live(t + 2):
                    wait(act, v_done, t + 3)
                    wait(act, pv_done, t - 1)
                    act.activation(v[:, pv_mod(u, 2, 4), :], ps_a[:, :], ACT.Copy).then_inc(v_copied, 1)
                copy_turned(2)
                copy_turned(3)
                exps(HEADS // 2, HEADS)
                b = t - 1
                if live(b):
                    wait(act, pv_done, b + 1)
                    wait(act, proj_done, b)
                    act.activation(oT_hi[:, :, :].rearrange("p c n -> p (c n)"), ps_c[:, :],
                                   ACT.Copy).then_inc(oT_rounded, 1)
                b = t - 4
                if live(b):
                    p2 = u % 2
                    wait(act, conv_done, b + 1)
                    if not isinstance(t, int) or b // 2 > 0:
                        wait(act, st_conv[p2], 16 * half(i, u, -4))
                    act.activation(conv[:, p2, :], ps_a[:, :], ACT.Copy).then_inc(conv_copied, 1)
                    wait(act, squares_added, b)
                    act.activation(square[:, :], ps_a[:, :], ACT.Square).then_inc(squared, 1)

            run_slots(act, slot, -2)

        @block.vector
        def _(dve):
            dve.memset(head_rows[:, :], 0.0).then_inc(rows_cleared, 1)
            dve.wait_ge(rows_cleared, 1)
            for h in range(HPC):
                dve.memset(head_rows[HD * h:HD * h + HD, h:h + 1], 1.0).then_inc(consts_set, 1)
            for i, k in enumerate("vqko"):
                dve.wait_ge(ld_w[i], 16)
                stage = prob[:, i % 2, :, :].rearrange("p h m -> p (h m)")
                hi = w_hi[k][:, :, :].rearrange("p c d -> p (c d)")
                dve.tensor_copy(hi, stage).then_inc(w_rounded, 1)
                dve.wait_ge(w_rounded, i + 1)
                dve.tensor_tensor(w_lo[k][:, :, :].rearrange("p c d -> p (c d)"), stage,
                                  hi.bitcast(F32), ALU.subtract).then_inc(w_split, 1)
            dve.wait_ge(w_split, 4)
            dve.wait_ge(pool_ready, READY)
            dve.wait_ge(ld_const, 48)

            def slot(i, u, live):
                t = i * 4 + u
                pair, par = half(i, u), u // 2
                b4 = t - 4
                if live(b4):
                    wait(dve, y_done, b4 + 1)
                    wait(dve, router_done, b4)
                    wait(dve, stats_added, b4)
                    dve.tensor_copy(sums[:, :, :].rearrange("p c k -> p (c k)"),
                                    ps_small[:, 0:2 * C]).then_inc(sums_copied, 1)

                def bias(c):
                    if live(t):
                        wait(dve, scores_done, C * t + c + 1)
                        if c == 0:
                            wait(dve, ld_adj[par], 16 * (quarter(i, u) + 1))
                            wait(dve, turned, C * (t - 1))
                        dve.scalar_tensor_tensor(
                            out=prob[:, u % 2, HPC * c:HPC * (c + 1), :],
                            in0=ps_scores[c % 2][:, :].rearrange("p (h m) -> p h m", h=HPC),
                            scalar=HALF_SCALE,
                            in1=adj_in[:, par, u % 2, :].unsqueeze(1).to_broadcast([P, HPC, P]),
                            op0=ALU.mult, op1=ALU.add).then_inc(biased, 1)

                bias(0)
                bias(1)
                b = t - 1
                if live(b):
                    p2 = pv_mod(u, -1, 2)
                    wait(dve, exp_done, b + 1)
                    dve.reciprocal(inv_sum[:, :], row_sum[:, p2, :]).then_inc(sum_inverted, 1)
                    wait(dve, sum_inverted, b + 1)
                    dve.scalar_tensor_tensor(out=inv_nz[:, :], in0=abs_max[:, p2, :], scalar=0.0,
                                             in1=inv_sum[:, :], op0=ALU.not_equal,
                                             op1=ALU.mult).then_inc(zero_rows_out, 1)
                    wait(dve, zero_rows_out, b + 1)
                    dve.tensor_tensor(prob[:, p2, :, :], prob[:, p2, :, :],
                                      inv_nz[:, :].unsqueeze(2).to_broadcast([P, HEADS, P]),
                                      ALU.mult).then_inc(normalised, 1)
                bias(2)
                bias(3)
                b = b4
                if live(b):
                    wait(dve, router_done, b + 1)
                    dve.tensor_tensor(logits[:, :], ps_small[:, 2 * C:2 * C + E], rb[:, :],
                                      ALU.add).then_inc(logits_made, 1)
                    wait(dve, logits_made, b + 1)
                    dve.tensor_reduce(top[:, :], logits[:, :], AX.X, ALU.max).then_inc(top_found, 1)
                    wait(dve, top_found, b + 1)
                    dve.scalar_tensor_tensor(out=ranked[:, :], in0=logits[:, :], scalar=top[:, :],
                                             in1=rank[:, :], op0=ALU.is_ge,
                                             op1=ALU.mult).then_inc(ranked_made, 1)
                    wait(dve, ranked_made, b + 1)
                    dve.tensor_reduce(best[:, :], ranked[:, :], AX.X, ALU.max).then_inc(best_found, 1)
                    wait(dve, best_found, b + 1)
                    dve.tensor_scalar(neg_best[:, :], best[:, :], 1.0, -1.0, ALU.max,
                                      ALU.mult).then_inc(best_negated, 1)
                    dve.tensor_scalar(one_hot[:, :], ranked[:, :], best[:, :], None,
                                      ALU.is_equal).then_inc(hot_made, 1)
                    wait(dve, best_negated, b + 1)
                    dve.tensor_scalar(expert_of[:, bass.ds(b, 1)], neg_best[:, :], float(E), None,
                                      ALU.add).then_inc(expert_known, 1)
                if live(t):
                    wait(dve, biased, C * (t + 1))
                    dve.tensor_reduce(neg_max[:, u % 2, :], prob[:, u % 2, :, :], AX.X, ALU.max,
                                      negate=True).then_inc(max_found, 1)
                    wait(dve, max_found, t + 1)
                    dve.tensor_scalar(neg_max2[:, u % 2, :], neg_max[:, u % 2, :], 2.0, None,
                                      ALU.mult).then_inc(max_doubled, 1)
                    dve.tensor_reduce(abs_max[:, u % 2, :], prob[:, u % 2, :, :], AX.X, ALU.max,
                                      apply_absolute_value=True).then_inc(abs_found, 1)
                if live(b4):
                    b = b4
                    wait(dve, hot_made, b + 1)
                    dve.tensor_tensor(count[:, :], count[:, :], one_hot[:, :], ALU.add)
                    dve.tensor_tensor(picked[:, :, :], one_hot[:, :].unsqueeze(2).to_broadcast([P, E, C]),
                                      sums[:, :, 0].unsqueeze(1).to_broadcast([P, E, C]),
                                      ALU.mult).then_inc(picked_made, 1)
                    wait(dve, picked_made, b + 1)
                    dve.tensor_tensor(conv_sum[:, :, :], conv_sum[:, :, :], picked[:, :, :],
                                      ALU.add).then_inc(stats_added, 1)
                b = t - 2
                if live(b):
                    p2 = u % 2
                    wait(dve, proj_done, b + 1)
                    wait(dve, ld_x[p2], 16 * (half(i, u, -2) + 1))
                    wait(dve, y_done, b - 1)
                    if not isinstance(t, int) or b // 2 > 0:
                        wait(dve, st_x1[p2], 16 * half(i, u, -2))
                    dve.tensor_tensor(x1[:, p2, :], ps_b[:, :], x_in[:, p2, :],
                                      ALU.add).then_inc(residual_added, 1)
                    wait(dve, residual_added, b + 1)
                    dve.bn_stats(stats[:, :], x1[:, p2, :]).then_inc(stats_taken, 1)
                    wait(dve, stats_taken, b + 1)
                b = t - 3
                if live(b):
                    p4 = pv_mod(u, -3, 4)
                    wait(dve, ld_adjT[p4 // 2], 16 * (quarter(i, u, -3) + 1))
                    wait(dve, y_done, b - 1)
                    dve.tensor_reduce(row_and_mean[:, p4 % 2, 0:1], adjT_in[:, p4 // 2, p4 % 2, :],
                                      AX.X, ALU.add).then_inc(rows_summed, 1)
                if live(t - 2):
                    dve.bn_aggr(mean_var[:, :], stats[:, :]).then_inc(stats_joined, 1)
                    b = t - 2
                    wait(dve, stats_joined, b + 1)
                    dve.tensor_scalar(var_eps[:, :], mean_var[:, 1:2], EPS, None,
                                      ALU.add).then_inc(var_ready, 1)
                b = t - 1
                if live(b):
                    wait(dve, oT_rounded, b + 1)
                    wait(dve, proj_done, b)
                    dve.tensor_tensor(oT_lo[:, :, :].rearrange("p c n -> p (c n)"), ps_c[:, :],
                                      oT_hi[:, :, :].rearrange("p c n -> p (c n)").bitcast(F32),
                                      ALU.subtract).then_inc(oT_split, 1)
                b = t - 2
                if live(b):
                    wait(dve, rstd_made, b + 1)
                    dve.tensor_scalar(x1[:, u % 2, :], x1[:, u % 2, :], mean_var[:, 0:1], rstd[:, :],
                                      ALU.subtract, ALU.mult).then_inc(x1_ready, 1)

            run_slots(dve, slot, -2)

        phase_one.close()
        p1.close()
        phase_two(nc, ctx, locals())


def phase_two(nc, ctx, v):
    (B, D, E, C, N) = (v[k] for k in ("B", "D", "E", "C", "N"))
    out, x1_dram, conv_dram = v["out"], v["x1_dram"], v["conv_dram"]
    minus_half = v["minus_half"]
    experts, ones, expert_of = v["experts"], v["ones"], v["expert_of"]
    square_sum, conv_sum, count, bank = v["square_sum"], v["conv_sum"], v["count"], v["bank"]
    G = 4
    NG = B // G
    RING = 2
    assert NG % RING == 0 and NG > RING

    def sb(name, shape, dt=F32):
        return ctx.enter_context(nc.sbuf_tensor(name, shape, dt))

    def sem(name):
        return ctx.enter_context(nc.semaphore(name))

    bn_scale = sb("bn_scale", [P, E * D])
    bn_shift = sb("bn_shift", [P, E * D])
    bn_mean = sb("bn_mean", [P, E * D])
    bn_square = sb("bn_square", [P, E * D])
    nodes = sb("nodes", [P, E])
    inv_nodes = sb("inv_nodes", [P, E])
    var_eps = sb("var_eps2", [P, G])
    conv_in = sb("conv_in", [P, RING, G, D])
    x1_in = sb("x1_in", [P, RING, G, D])
    stats = sb("stats2", [P, G, 6])
    mean_var = sb("mean_var2", [P, G, 2])
    rstd = sb("rstd2", [P, G])
    shift = sb("shift2", [P, G])

    ld_bn = sem("ld_bn")
    ld_g = [sem(f"ld_g{i}") for i in range(RING)]
    st_g = [sem(f"st_g{i}") for i in range(RING)]
    summed = sem("summed")
    var_known = sem("var_known")
    dve_passed = sem("dve_passed")
    inverted = sem("inverted")
    var_ready = sem("var_ready2")
    table_step = sem("table_step")
    table_ready = sem("table_ready")
    scaled = sem("scaled")
    shifted = sem("shifted")
    joined = sem("joined")
    stats_taken = sem("stats_taken2")
    stats_joined = sem("stats_joined2")
    rstd_made = sem("rstd_made2")
    shift_made = sem("shift_made2")
    finished = sem("finished")

    def run_groups(eng, group):
        for r in range(RING):
            group(0, r)
        with eng.Fori(1, NG // RING, 1) as k:
            for r in range(RING):
                group(k, r)

    block = ctx.enter_context(nc.Block())

    @block.sync
    def _(sp):
        sp.dma_start(bn_scale[:, :], v["gamma"].partition_broadcast(P)).then_inc(ld_bn, 16)
        sp.dma_start(bn_shift[:, :], v["beta"].partition_broadcast(P)).then_inc(ld_bn, 16)

        def load(k, r):
            g = k * RING + r
            if not isinstance(k, int):
                sp.wait_ge(st_g[r], k * 16)
            sp.dma_start(conv_in[:, r, :, :], conv_dram[:, bass.ds(g * G, G), :]).then_inc(ld_g[r], 16)
            sp.dma_start(x1_in[:, r, :, :], x1_dram[:, bass.ds(g * G, G), :]).then_inc(ld_g[r], 16)

        run_groups(sp, load)

    @block.gpsimd
    def _(pool):
        for e in range(E):
            pool.wait_ge(var_known, e + 1)
            sq = bn_square[:, e * D:(e + 1) * D]
            pool.tensor_tensor(sq, sq, minus_half[:, :].to_broadcast([P, D]), ALU.pow).then_inc(inverted, 1)
        pool.wait_ge(table_ready, 1)

        def group(k, r):
            g = k * RING + r
            pool.wait_ge(ld_g[r], (k + 1) * 32)
            for j in range(G):
                e = pool.value_load(expert_of[0:1, bass.ds(g * G + j, 1)], min_val=0, max_val=E - 1)
                pool.tensor_tensor(conv_in[:, r, j, :], conv_in[:, r, j, :],
                                   bn_scale[:, bass.ds(e * D, D)], ALU.mult).then_inc(scaled, 1)
            if not isinstance(g, int) or g > 0:
                root(g - 1)

        def root(g):
            pool.wait_ge(var_ready, g + 1)
            pool.tensor_tensor(rstd[:, :], var_eps[:, :], minus_half[:, :].to_broadcast([P, G]), ALU.pow).then_inc(rstd_made, 1)

        run_groups(pool, group)
        root(NG - 1)

    @block.tensor
    def _(pe):
        for e in range(E):
            last = pe.matmul(bank[e][:, :], ones[:, :], square_sum[:, e * D:(e + 1) * D],
                             start=True, stop=True)
        for e in range(E):
            for c in range(C):
                last = pe.matmul(bank[E + e][:, :], conv_sum[:, e, c:c + 1].to_broadcast([P, P]),
                                 experts[:, (e * C + c) * D:(e * C + c + 1) * D],
                                 start=(c == 0), stop=(c == C - 1))
        last.then_inc(summed, 1)

    @block.scalar
    def _(act):
        def group(k, r):
            g = k * RING + r
            for j in range(G):
                if j == 0:
                    act.wait_ge(shift_made, g + 1)
                last = act.activation(x1_in[:, r, j, :], x1_in[:, r, j, :], ACT.Identity,
                                      bias=shift[:, j:j + 1], scale=rstd[:, j:j + 1])
            last.then_inc(finished, 1)
            act.wait_ge(finished, g + 1)
            act.dma_start(out[bass.ds(g * G, G), :, :].rearrange("b n d -> n b d"),
                          x1_in[:, r, :, :]).then_inc(st_g[r], 16)

        run_groups(act, group)
        for r in range(RING):
            act.wait_ge(st_g[r], 16 * (NG // RING))

    @block.vector
    def _(dve):
        steps = [0]

        def step(ins):
            steps[0] += 1
            ins.then_inc(table_step, 1)
            dve.wait_ge(table_step, steps[0])

        step(dve.tensor_scalar(nodes[:, :], count[:, :], float(N), 1.0, ALU.mult, ALU.max))
        step(dve.reciprocal(inv_nodes[:, :], nodes[:, :]))
        dve.wait_ge(summed, 1)
        dve.wait_ge(ld_bn, 32)
        cols = [slice(e * D, (e + 1) * D) for e in range(E)]
        for e in range(E):
            mean, sq = bn_mean[:, cols[e]], bn_square[:, cols[e]]
            step(dve.tensor_scalar(mean, bank[E + e][:, :], inv_nodes[:, e:e + 1], None, ALU.mult))
            step(dve.tensor_tensor(sq, mean, mean, ALU.mult))
            step(dve.scalar_tensor_tensor(out=sq, in0=bank[e][:, :], scalar=inv_nodes[:, e:e + 1], in1=sq,
                                          op0=ALU.mult, op1=ALU.subtract))
            dve.tensor_scalar(sq, sq, EPS, None, ALU.add).then_inc(var_known, 1)
        for e in range(E):
            mean, sq, sc, sh = bn_mean[:, cols[e]], bn_square[:, cols[e]], bn_scale[:, cols[e]], bn_shift[:, cols[e]]
            dve.wait_ge(inverted, e + 1)
            step(dve.tensor_tensor(sc, sc, sq, ALU.mult))
            step(dve.tensor_tensor(mean, mean, sc, ALU.mult))
            step(dve.tensor_tensor(sh, sh, mean, ALU.subtract))
        dve.nop().then_inc(table_ready, 1)

        def group(k, r):
            g = k * RING + r
            for j in range(G):
                n = g * G + j
                e = dve.value_load(expert_of[0:1, bass.ds(n, 1)], min_val=0, max_val=E - 1)
                dve.wait_ge(scaled, n + 1)
                dve.tensor_tensor(conv_in[:, r, j, :], conv_in[:, r, j, :],
                                  bn_shift[:, bass.ds(e * D, D)], ALU.add).then_inc(shifted, 1)
                dve.wait_ge(shifted, n + 1)
                dve.scalar_tensor_tensor(out=x1_in[:, r, j, :], in0=conv_in[:, r, j, :], scalar=0.0,
                                         in1=x1_in[:, r, j, :], op0=ALU.max,
                                         op1=ALU.add).then_inc(joined, 1)
                dve.wait_ge(joined, n + 1)
                dve.bn_stats(stats[:, j, :], x1_in[:, r, j, :]).then_inc(stats_taken, 1)
            dve.wait_ge(stats_taken, (g + 1) * G)
            dve.sem_inc(dve_passed)
            for j in range(G):
                dve.bn_aggr(mean_var[:, j, :], stats[:, j, :]).then_inc(stats_joined, 1)
            dve.wait_ge(stats_joined, (g + 1) * G)
            if not isinstance(g, int) or g > 0:
                dve.wait_ge(finished, g)
            dve.tensor_scalar(var_eps[:, :], mean_var[:, :, 1], EPS, None, ALU.add).then_inc(var_ready, 1)
            dve.wait_ge(rstd_made, g + 1)
            dve.scalar_tensor_tensor(out=shift[:, :], in0=mean_var[:, :, 0], scalar=-1.0, in1=rstd[:, :],
                                     op0=ALU.mult, op1=ALU.mult).then_inc(shift_made, 1)

        run_groups(dve, group)


def kernel(x, adj, L0_gnn_Wq, L0_gnn_Wk, L0_gnn_Wv, L0_gnn_Wo, L1_gnn_router_w, L1_gnn_router_b,
           L1_gnn_expert_w, L1_gnn_bn_gamma, L1_gnn_bn_beta):
    import numpy as np
    import concourse.bacc as bacc
    from concourse.bass_utils import run_bass_kernel_spmd

    x, adj = np.asarray(x), np.asarray(adj)
    B, N, D = x.shape
    E = L1_gnn_bn_gamma.shape[0]
    C = D // P

    def weight(w):
        w = np.asarray(w).T.reshape(C, P, D)
        return w.transpose(1, 0, 2).reshape(P, C * D)

    arrays = {
        "x": x,
        "xT": x.reshape(B // 2, 2 * N, C, P).transpose(3, 0, 2, 1).reshape(P, B // 2, C * 2 * N),
        "adj": adj,
        "adjT": adj.transpose(2, 0, 1),
        "wqT": weight(L0_gnn_Wq), "wkT": weight(L0_gnn_Wk),
        "wvT": weight(L0_gnn_Wv), "woT": weight(L0_gnn_Wo),
        "router_w": np.asarray(L1_gnn_router_w).reshape(C, P, E).transpose(1, 0, 2),
        "router_b": np.asarray(L1_gnn_router_b),
        "expert_w": np.asarray(L1_gnn_expert_w).reshape(E, C, P, D).transpose(2, 0, 1, 3).reshape(P, E * C * D),
        "gamma": np.asarray(L1_gnn_bn_gamma).reshape(E * D),
        "beta": np.asarray(L1_gnn_bn_beta).reshape(E * D),
    }
    arrays = {k: np.ascontiguousarray(a) for k, a in arrays.items()}
    nc = bacc.Bacc("TRN2", target_bir_lowering=False, num_devices=1)
    ins = [nc.dram_tensor(k, a.shape, F32, kind="ExternalInput").ap() for k, a in arrays.items()]
    out = nc.dram_tensor("out", (B, N, D), F32, kind="ExternalOutput").ap()
    graph_block_program(nc, *ins, out)
    r = run_bass_kernel_spmd(nc, [arrays], core_ids=[0])
    return r.results[0]["out"]
```

```python
from contextlib import ExitStack

import concourse.bass as bass
from concourse import mybir
from concourse.alu_op_type import AluOpType as ALU

F32 = mybir.dt.float32
F32R = mybir.dt.float32r
I32 = mybir.dt.int32
ACT = mybir.ActivationFunctionType
AX = mybir.AxisListType

P = 128
HEADS = 16
EPS = 1e-5


def graph_block_program(nc, x, xT, adj, adjT, wqT, wkT, wvT, woT, router_w, router_b, expert_w,
                        gamma, beta, out):
    B, N, D = x.shape
    E = router_w.shape[2]
    C = D // P
    HPC = HEADS // C
    HD = D // HEADS
    HALF_SCALE = 0.5 * float(D) ** -0.5
    assert N == P and HD == 32 and B % 4 == 0 and B >= 20

    x1_dram = nc.dram_tensor("x1_scratch", (P, B, D), F32, kind="Internal").ap()
    expert_hi_dram = nc.dram_tensor("expert_hi_scratch", (E, P, C, D), F32, kind="Internal").ap()
    expert_lo_dram = nc.dram_tensor("expert_lo_scratch", (E, P, C, D), F32, kind="Internal").ap()
    conv_dram = nc.dram_tensor("conv_scratch", (P, B, D), F32, kind="Internal").ap()

    with ExitStack() as ctx:
        def sem(name):
            return ctx.enter_context(nc.semaphore(name))

        expert_of = ctx.enter_context(nc.sbuf_tensor("expert_of", [P, B], I32))
        square_sum = ctx.enter_context(nc.sbuf_tensor("square_sum", [P, E * D], F32))
        conv_sum = ctx.enter_context(nc.sbuf_tensor("conv_sum", [P, E, C], F32))
        count = ctx.enter_context(nc.sbuf_tensor("count", [P, E], F32))
        minus_half = ctx.enter_context(nc.sbuf_tensor("minus_half", [P, 1], F32))
        ident = ctx.enter_context(nc.sbuf_tensor("ident", [P, P], F32))
        ones = ctx.enter_context(nc.sbuf_tensor("ones", [P, 1], F32))
        bank = [ctx.enter_context(nc.psum_tensor(f"bank{i}", [P, 512], F32)) for i in range(8)]
        ps_scores, ps_turned = bank[0:2], bank[2:4]
        ps_a, ps_b, ps_c, ps_small = bank[4:8]

        p1 = ExitStack()

        def sb(name, shape, dt=F32):
            return p1.enter_context(nc.sbuf_tensor(name, shape, dt))

        w_hi = {k: sb(f"w{k}_hi", [P, C, D], F32R) for k in "qkvo"}
        w_lo = {k: sb(f"w{k}_lo", [P, C, D], F32R) for k in "qkvo"}
        xT_in = sb("xT_in", [P, C, 2 * P])
        xT_hi = sb("xT_hi", [P, 2, C, 2 * P], F32R)
        xT_lo = sb("xT_lo", [P, 2, C, 2 * P], F32R)
        x_in = sb("x_in", [P, 2, D])
        adj_in = sb("adj_in", [P, 2, 2, P])
        adjT_in = sb("adjT_in", [P, 2, 2, P + 2])
        qk = sb("qk", [P, 2, C, 2, 2 * P])
        v = sb("v", [P, 4, D])
        k_diag = sb("k_diag", [P, C, HPC, P])
        prob = sb("prob", [P, 2, HEADS, P])
        probT = sb("probT", [P, HEADS, P])
        oT_hi = sb("oT_hi", [P, C, P], F32R)
        oT_lo = sb("oT_lo", [P, C, P], F32R)
        x1 = sb("x1", [P, 2, D])
        yT_hi = sb("yT_hi", [P, C, P], F32R)
        yT_lo = sb("yT_lo", [P, C, P], F32R)
        expert_hi = sb("expert_hi", [P, C, D], F32R)
        expert_lo = sb("expert_lo", [P, C, D], F32R)
        conv = sb("conv", [P, 2, D])
        square = sb("square", [P, D])
        head_rows = sb("head_rows", [P, HPC])
        rw = sb("rw", [P, C, E])
        rb = sb("rb", [P, E])
        neg_max = sb("neg_max", [P, 2, HEADS])
        neg_max2 = sb("neg_max2", [P, 2, HEADS])
        abs_max = sb("abs_max", [P, 2, HEADS])
        row_sum = sb("row_sum", [P, 2, HEADS])
        inv_sum = sb("inv_sum", [P, HEADS])
        inv_nz = sb("inv_nz", [P, HEADS])
        stats = sb("stats", [P, 6])
        mean_var = sb("mean_var", [P, 2])
        var_eps = sb("var_eps", [P, 1])
        rstd = sb("rstd", [P, 1])
        sums = sb("sums", [P, C, 2])
        logits = sb("logits", [P, E])
        top = sb("top", [P, 1])
        rank = sb("rank", [P, E])
        ranked = sb("ranked", [P, E])
        best = sb("best", [P, 1])
        neg_best = sb("neg_best", [P, 1])
        one_hot = sb("one_hot", [P, E])
        picked = sb("picked", [P, E, C])

        ld_w = [sem(f"ld_w{i}") for i in range(4)]
        ld_const = sem("ld_const")
        ld_expert = [sem("ld_expert0"), sem("ld_expert1")]
        st_expert = sem("st_expert")
        ld_hi = sem("ld_hi")
        ld_lo = sem("ld_lo")
        ld_xT = sem("ld_xT")
        ld_x = [sem("ld_x0"), sem("ld_x1")]
        ld_adj = [sem("ld_adj0"), sem("ld_adj1")]
        ld_adjT = [sem("ld_adjT0"), sem("ld_adjT1")]
        st_x1 = [sem("st_x1_0"), sem("st_x1_1")]
        st_conv = [sem("st_conv0"), sem("st_conv1")]
        pool_zeroed = sem("pool_zeroed")
        pool_ready = sem("pool_ready")
        pool_passed = sem("pool_passed")
        x_split = sem("x_split")
        x_rounded = sem("x_rounded")
        diag_built = sem("diag_built")
        squares_added = sem("squares_added")
        rstd_made = sem("rstd_made")
        scores_done = sem("scores_done")
        qk_done = sem("qk_done")
        v_done = sem("v_done")
        turned = sem("turned")
        pv_done = sem("pv_done")
        proj_done = sem("proj_done")
        y_done = sem("y_done")
        router_done = sem("router_done")
        conv_done = sem("conv_done")
        qk_copied = sem("qk_copied")
        v_copied = sem("v_copied")
        probT_copied = sem("probT_copied")
        exp_done = sem("exp_done")
        oT_rounded = sem("oT_rounded")
        y_rounded = sem("y_rounded")
        conv_copied = sem("conv_copied")
        squared = sem("squared")
        w_rounded = sem("w_rounded")
        w_split = sem("w_split")
        rows_cleared = sem("rows_cleared")
        consts_set = sem("consts_set")
        biased = sem("biased")
        max_found = sem("max_found")
        max_doubled = sem("max_doubled")
        abs_found = sem("abs_found")
        sum_inverted = sem("sum_inverted")
        zero_rows_out = sem("zero_rows_out")
        normalised = sem("normalised")
        oT_split = sem("oT_split")
        residual_added = sem("residual_added")
        stats_taken = sem("stats_taken")
        stats_joined = sem("stats_joined")
        var_ready = sem("var_ready")
        x1_ready = sem("x1_ready")
        rows_summed = sem("rows_summed")
        sums_copied = sem("sums_copied")
        y_split = sem("y_split")
        expert_rounded = sem("expert_rounded")
        expert_split = sem("expert_split")
        logits_made = sem("logits_made")
        top_found = sem("top_found")
        ranked_made = sem("ranked_made")
        best_found = sem("best_found")
        best_negated = sem("best_negated")
        hot_made = sem("hot_made")
        expert_known = sem("expert_known")
        picked_made = sem("picked_made")
        stats_added = sem("stats_added")

        SLOT_LOOP_START, SLOT_LOOP_END, SLOT_END = 8, B - 8, B + 5

        def run_slots(eng, slot, first):
            for t in range(first, SLOT_LOOP_START):
                slot(t // 4, t % 4, lambda b: 0 <= b < B)
            with eng.Fori(SLOT_LOOP_START // 4, SLOT_LOOP_END // 4, 1) as i:
                for u in range(4):
                    slot(i, u, lambda b: True)
            for t in range(SLOT_LOOP_END, SLOT_END):
                slot(t // 4, t % 4, lambda b: 0 <= b < B)

        def wait(eng, s, value):
            if not isinstance(value, int) or value > 0:
                eng.wait_ge(s, value)

        def half(i, u, k=0):
            return i * 2 + (u + k) // 2

        def quarter(i, u, k=0):
            return i + (u + k) // 4

        def pv_mod(u, k, m):
            return (u + k) % m

        Y = P + 2
        READY = 7 + E

        phase_one = ExitStack()
        block = phase_one.enter_context(nc.Block())

        @block.sync
        def _(sp):
            def load_xT(pair):
                wait(sp, x_split, pair)
                sp.dma_start(xT_in[:, :, :], xT[:, bass.ds(pair, 1), :].rearrange(
                    "p g (c n) -> p (g c) n", c=C)).then_inc(ld_xT, 16)

            def store_expert(e):
                sp.wait_ge(expert_split, e + 1)
                sp.dma_start(expert_hi_dram[e, :, :, :], expert_hi[:, :, :].bitcast(F32)).then_inc(st_expert, 16)
                sp.dma_start(expert_lo_dram[e, :, :, :], expert_lo[:, :, :].bitcast(F32)).then_inc(st_expert, 16)

            for i, (k, w) in enumerate(zip("vqko", (wvT, wqT, wkT, woT))):
                if i == 1:
                    load_xT(0)
                if i >= 2:
                    sp.wait_ge(w_split, i - 1)
                sp.dma_start(prob[:, i % 2, :, :].rearrange("p h m -> p (h m)"),
                             w).then_inc(ld_w[i], 16)
            for dst, src in ((rw[:, :, :], router_w), (rb[:, :], router_b.partition_broadcast(P))):
                sp.dma_start(dst, src).then_inc(ld_const, 16)
            for e in range(E):
                sp.wait_ge(w_split, 3 + e if e < 2 else 4)
                if e >= 2:
                    sp.wait_ge(expert_split, e - 1)
                sp.dma_start(prob[:, e % 2, :, :].rearrange("p h m -> p (h m)"),
                             expert_w[:, e * C * D:(e + 1) * C * D]).then_inc(ld_expert[e % 2], 16)
                if e >= 1:
                    store_expert(e - 1)
            store_expert(E - 1)

            def slot(i, u, live):
                t = i * 4 + u
                b = t - 3
                if live(b):
                    wait(sp, x1_ready, b + 1)
                    par = pv_mod(u, -3, 2)
                    sp.dma_start(x1_dram[:, bass.ds(b, 1), :].rearrange("p b d -> p (b d)"),
                                 x1[:, par, :]).then_inc(st_x1[par], 16)
                b = t - 5
                if live(b):
                    wait(sp, conv_copied, b + 1)
                    par = pv_mod(u, -5, 2)
                    sp.dma_start(conv_dram[:, bass.ds(b, 1), :].rearrange("p b d -> p (b d)"),
                                 conv[:, par, :]).then_inc(st_conv[par], 16)
                if u % 2 == 0:
                    g = half(i, u)
                    pair = g + 1
                    if live(2 * pair):
                        par = (u // 2 + 1) % 2
                        wait(sp, biased, 8 * g)
                        sp.dma_start(adj_in[:, par, :, :], adj[bass.ds(2 * pair, 2), :, :].rearrange(
                            "b n m -> n b m")).then_inc(ld_adj[par], 16)
                    pair = g - 1
                    if live(2 * pair):
                        par = (u // 2 + 1) % 2
                        wait(sp, y_done, 2 * g - 4)
                        sp.dma_start(adjT_in[:, par, :, 0:P], adjT[:, bass.ds(2 * pair, 2), :]
                                     ).then_inc(ld_adjT[par], 16)
                b = t - 4
                if live(b):
                    wait(sp, expert_known, b + 1)
                    e = sp.value_load(expert_of[0:1, bass.ds(b, 1)], min_val=0, max_val=E - 1)
                    if isinstance(b, int) and b == 0:
                        sp.wait_ge(st_expert, 32 * E)
                    wait(sp, conv_done, b)
                    sp.dma_start(expert_hi[:, :, :].bitcast(F32), expert_hi_dram[bass.ds(e, 1), :, :, :].rearrange(
                        "e p c d -> p (e c) d")).then_inc(ld_hi, 16)
                    sp.dma_start(expert_lo[:, :, :].bitcast(F32), expert_lo_dram[bass.ds(e, 1), :, :, :].rearrange(
                        "e p c d -> p (e c) d")).then_inc(ld_lo, 16)
                if live(t):
                    wait(sp, residual_added, t - 1)
                    sp.dma_start(x_in[:, u % 2, :], x[bass.ds(t, 1), :, :].rearrange(
                        "b n d -> n (b d)")).then_inc(ld_x[u % 2], 16)
                if u % 2 == 0:
                    g = half(i, u)
                    if live(2 * (g + 3)) and (not isinstance(t, int) or g + 3 > 0):
                        load_xT(g + 3)

            run_slots(sp, slot, -4)
            for par in range(2):
                sp.wait_ge(st_x1[par], 16 * (B // 2))
                sp.wait_ge(st_conv[par], 16 * (B // 2))

        @block.gpsimd
        def _(pool):
            pool.memset(ident[:, :], 0.0).then_inc(pool_zeroed, 1)
            pool.memset(square_sum[:, :], 0.0).then_inc(pool_ready, 1)
            pool.memset(conv_sum[:, :, :], 0.0).then_inc(pool_ready, 1)
            pool.memset(count[:, :], 0.0).then_inc(pool_ready, 1)
            pool.memset(adjT_in[:, :, :, P + 1:P + 2], 1.0 / N).then_inc(pool_ready, 1)
            pool.memset(ones[:, :], 1.0).then_inc(pool_ready, 1)
            pool.memset(minus_half[:, :], -0.5).then_inc(pool_ready, 1)
            for e in range(E):
                pool.memset(rank[:, e:e + 1], float(E - e)).then_inc(pool_ready, 1)
            pool.wait_ge(pool_zeroed, 1)
            pool.affine_select(out=ident[:, :], in_=ident[:, :], compare_op=ALU.not_equal, fill=1.0,
                               base=0, pattern=[[-1, P]], channel_multiplier=1).then_inc(pool_ready, 1)
            pool.wait_ge(pool_ready, READY - 1)

            def split_xT(pair, par):
                wait(pool, ld_xT, 16 * (pair + 1))
                wait(pool, v_done, 2 * pair - 2)
                wait(pool, qk_done, C * (pair - 1))
                pool.sem_inc(pool_passed)
                pool.tensor_copy(xT_hi[:, par, :, :], xT_in[:, :, :]).then_inc(x_rounded, 1)
                wait(pool, x_rounded, pair + 1)
                pool.tensor_tensor(xT_lo[:, par, :, :], xT_in[:, :, :],
                                   xT_hi[:, par, :, :].bitcast(F32), ALU.subtract).then_inc(x_split, 1)

            def slot(i, u, live):
                t = i * 4 + u
                if u % 2 == 0:
                    pair = half(i, u) + 2
                    if live(2 * pair):
                        split_xT(pair, (u // 2) % 2)
                if live(t - 2):
                    wait(pool, var_ready, t - 1)
                    pool.tensor_tensor(rstd[:, :], var_eps[:, :], minus_half[:, 0:1],
                                       ALU.pow).then_inc(rstd_made, 1)
                b = t - 4
                if live(b):
                    wait(pool, expert_known, b + 1)
                    e = pool.value_load(expert_of[0:1, bass.ds(b, 1)], min_val=0, max_val=E - 1)
                    wait(pool, squared, b + 1)
                    wait(pool, squares_added, b)
                    acc = square_sum[:, bass.ds(e * D, D)]
                    pool.tensor_tensor(acc, acc, square[:, :], ALU.add).then_inc(squares_added, 1)

            run_slots(pool, slot, -4)

        @block.tensor
        def _(pe):
            def mm(dst, lhsT, rhs, start, stop):
                return pe.matmul(dst, lhsT, rhs, start=start, stop=stop)

            def mm3(dst, lhs, rhs):
                n = len(lhs)
                for i, ((lh, ll), (rh, rl)) in enumerate(zip(lhs, rhs)):
                    mm(dst, lh, rh, i == 0, False)
                    mm(dst, lh, rl, False, False)
                    last = mm(dst, ll, rh, False, i == n - 1)
                return last

            pe.wait_ge(pool_ready, READY)
            pe.wait_ge(w_split, 3)

            def slot(i, u, live):
                t = i * 4 + u
                pair = half(i, u)
                par = u // 2

                def scores(c):
                    b = t
                    if not live(b):
                        return
                    if c == 0:
                        wait(pe, qk_copied, C * (pair + 1))
                        wait(pe, diag_built, b + 1)
                    wait(pe, biased, C * b + c - 1)
                    side = u % 2
                    mm(ps_scores[c % 2][:, :], qk[:, par, c, 0, side * P:side * P + P],
                       k_diag[:, c, :, :].rearrange("p h m -> p (h m)"), True, True
                       ).then_inc(scores_done, 1)

                def project_qk(c, dst):
                    nxt, npar = pair + 1, (par + 1) % 2
                    if not live(2 * nxt):
                        return
                    wait(pe, x_split, nxt + 1)
                    for i, k in enumerate("qk"):
                        last = mm3(dst[:, i * 2 * P:(i + 1) * 2 * P],
                                   [(w_hi[k][:, j, c * P:(c + 1) * P], w_lo[k][:, j, c * P:(c + 1) * P])
                                    for j in range(C)],
                                   [(xT_hi[:, npar, j, :], xT_lo[:, npar, j, :]) for j in range(C)])
                    last.then_inc(qk_done, 1)

                def turn(c):
                    b = t - 1
                    if not live(b):
                        return
                    if c == 0:
                        wait(pe, normalised, b + 1)
                    wait(pe, probT_copied, C * b + c - 1)
                    for h in range(HPC):
                        last = pe.transpose(ps_turned[c % 2][:, h * P:(h + 1) * P],
                                            prob[:, pv_mod(u, -1, 2), HPC * c + h, :], ident[:, :])
                    last.then_inc(turned, 1)

                def times_v(c):
                    b = t - 1
                    if not live(b):
                        return
                    if c == 0:
                        wait(pe, v_copied, b + 1)
                        wait(pe, y_split, b - 2)
                    wait(pe, probT_copied, C * b + c + 1)
                    for h in range(HPC):
                        col = (HPC * c + h) * HD
                        last = mm(ps_c[HD * h:HD * h + HD, c * P:(c + 1) * P],
                                  v[:, pv_mod(u, -1, 4), col:col + HD], probT[:, HPC * c + h, :], True, True)
                    if c == C - 1:
                        last.then_inc(pv_done, 1)

                scores(0)
                scores(1)
                b5 = t - 5
                if live(2 * (pair + 1)):
                    if live(b5):
                        wait(pe, squared, b5 + 1)
                    else:
                        wait(pe, v_copied, t + 2)
                project_qk((2 * u) % C, ps_a)
                b = t - 4
                if live(b):
                    if isinstance(b, int) and b == 0:
                        pe.wait_ge(ld_const, 32)
                    wait(pe, y_split, b + 1)
                    for c in range(C):
                        last = mm(ps_small[:, P + 2:P + 2 + E], sums[:, c, 1:2].to_broadcast([P, P]),
                                  rw[:, c, :], c == 0, c == C - 1)
                    last.then_inc(router_done, 1)
                scores(2)
                scores(3)
                if live(2 * (pair + 1)):
                    if live(t - 3):
                        wait(pe, residual_added, t - 2)
                    else:
                        wait(pe, qk_copied, C * (pair + 1) + (2 * u) % C)
                project_qk((2 * u) % C + 1, ps_b)
                turn(0)
                turn(1)
                b = t + 2
                if live(b):
                    nxt, npar = pair + 1, (par + 1) % 2
                    wait(pe, qk_copied, C * nxt + (2 * u) % C + 1)
                    mm3(ps_a[:, :],
                        [(xT_hi[:, npar, j, u % 2 * P:u % 2 * P + P], xT_lo[:, npar, j, u % 2 * P:u % 2 * P + P])
                         for j in range(C)],
                        [(w_hi["v"][:, j, :], w_lo["v"][:, j, :]) for j in range(C)]).then_inc(v_done, 1)
                turn(2)
                turn(3)
                times_v(0)
                times_v(1)
                b = t - 2
                if live(b):
                    wait(pe, oT_split, b + 1)
                    if isinstance(b, int) and b == 0:
                        pe.wait_ge(w_split, 4)
                    if live(2 * (pair + 1)):
                        wait(pe, qk_copied, C * (pair + 1) + (2 * u) % C + 2)
                    else:
                        wait(pe, residual_added, b)
                    mm3(ps_b[:, :], [(oT_hi[:, j, :], oT_lo[:, j, :]) for j in range(C)],
                        [(w_hi["o"][:, j, :], w_lo["o"][:, j, :]) for j in range(C)]).then_inc(proj_done, 1)
                times_v(2)
                times_v(3)
                b = t - 4
                if live(b):
                    wait(pe, y_split, b + 1)
                    if live(t + 2):
                        wait(pe, v_copied, t + 3)
                    else:
                        wait(pe, squared, b)
                    wait(pe, ld_hi, (b + 1) * 16)
                    for c in range(C):
                        mm(ps_a[:, :], yT_hi[:, c, :], expert_hi[:, c, :], c == 0, False)
                        mm(ps_a[:, :], yT_lo[:, c, :], expert_hi[:, c, :], False, False)
                    wait(pe, ld_lo, (b + 1) * 16)
                    for c in range(C):
                        last = mm(ps_a[:, :], yT_hi[:, c, :], expert_lo[:, c, :], False, c == C - 1)
                    last.then_inc(conv_done, 1)
                b = t - 3
                if live(b):
                    p4 = pv_mod(u, -3, 4)
                    wait(pe, x1_ready, b + 1)
                    wait(pe, rows_summed, b + 1)
                    if live(t - 1):
                        wait(pe, oT_split, t)
                    else:
                        wait(pe, y_split, b)
                    wait(pe, expert_known, b)
                    for c in range(C):
                        lhsT = x1[:, p4 % 2, c * P:(c + 1) * P]
                        dst = ps_c[:, c * Y:(c + 1) * Y] if c < C - 1 else ps_small[:, 0:Y]
                        last = mm(dst, lhsT, adjT_in[:, p4 // 2, p4 % 2, :], True, True)
                    last.then_inc(y_done, 1)

            run_slots(pe, slot, -2)

        @block.scalar
        def _(act):
            def slot(i, u, live):
                t = i * 4 + u
                pair, par = half(i, u), u // 2
                nxt, npar = pair + 1, (par + 1) % 2
                b = t - 4
                if live(b):
                    wait(act, y_done, b + 1)
                    wait(act, conv_done, b)
                    act.activation(yT_hi[:, 0:C - 1, :], ps_c[:, 0:(C - 1) * Y].rearrange(
                        "p (c n) -> p c n", c=C - 1)[:, :, 0:P], ACT.Copy)
                    act.activation(yT_hi[:, C - 1, :], ps_small[:, 0:P], ACT.Copy).then_inc(y_rounded, 1)

                def copy_qk(c, src):
                    if live(2 * nxt):
                        wait(act, qk_done, C * nxt + c + 1)
                        wait(act, scores_done, 2 * C * (nxt - 1))
                        act.activation(qk[:, npar, c, :, :].rearrange("p k n -> p (k n)"), src[:, :],
                                       ACT.Copy).then_inc(qk_copied, 1)

                def copy_turned(c):
                    if live(t - 1):
                        wait(act, turned, C * (t - 1) + c + 1)
                        wait(act, pv_done, t - 1)
                        act.activation(probT[:, HPC * c:HPC * (c + 1), :].rearrange("p h n -> p (h n)"),
                                       ps_turned[c % 2][:, :], ACT.Copy).then_inc(probT_copied, 1)

                copy_qk((2 * u) % C, ps_a)
                copy_qk((2 * u) % C + 1, ps_b)
                copy_turned(0)
                copy_turned(1)
                if live(t + 2):
                    wait(act, v_done, t + 3)
                    wait(act, pv_done, t - 1)
                    act.activation(v[:, pv_mod(u, 2, 4), :], ps_a[:, :], ACT.Copy).then_inc(v_copied, 1)
                copy_turned(2)
                copy_turned(3)

                def exps(h0, h1):
                    if live(t):
                        for h in range(h0, h1):
                            last = act.activation(prob[:, u % 2, h, :], prob[:, u % 2, h, :], ACT.Exp,
                                                  bias=neg_max2[:, u % 2, h:h + 1], scale=2.0,
                                                  accum_out=row_sum[:, u % 2, h:h + 1])
                        if h1 == HEADS:
                            last.then_inc(exp_done, 1)

                if live(t):
                    wait(act, abs_found, t + 1)
                    wait(act, max_doubled, t + 1)
                exps(0, 10)
                b = t - 1
                if live(b):
                    wait(act, pv_done, b + 1)
                    wait(act, proj_done, b)
                    act.activation(oT_hi[:, :, :].rearrange("p c n -> p (c n)"), ps_c[:, :],
                                   ACT.Copy).then_inc(oT_rounded, 1)
                exps(10, HEADS)
                b = t - 4
                if live(b):
                    p2 = u % 2
                    wait(act, conv_done, b + 1)
                    if not isinstance(t, int) or b // 2 > 0:
                        wait(act, st_conv[p2], 16 * half(i, u, -4))
                    act.activation(conv[:, p2, :], ps_a[:, :], ACT.Copy).then_inc(conv_copied, 1)
                    wait(act, squares_added, b)
                    act.activation(square[:, :], ps_a[:, :], ACT.Square).then_inc(squared, 1)

            run_slots(act, slot, -2)

        @block.vector
        def _(dve):
            dve.memset(head_rows[:, :], 0.0).then_inc(rows_cleared, 1)
            dve.wait_ge(rows_cleared, 1)
            for h in range(HPC):
                dve.memset(head_rows[HD * h:HD * h + HD, h:h + 1], 1.0).then_inc(consts_set, 1)
            for i, k in enumerate("vqko"):
                dve.wait_ge(ld_w[i], 16)
                stage = prob[:, i % 2, :, :].rearrange("p h m -> p (h m)")
                hi = w_hi[k][:, :, :].rearrange("p c d -> p (c d)")
                dve.tensor_copy(hi, stage).then_inc(w_rounded, 1)
                dve.wait_ge(w_rounded, i + 1)
                dve.tensor_tensor(w_lo[k][:, :, :].rearrange("p c d -> p (c d)"), stage,
                                  hi.bitcast(F32), ALU.subtract).then_inc(w_split, 1)
            for e in range(E):
                dve.wait_ge(ld_expert[e % 2], 16 * (e // 2 + 1))
                if e:
                    dve.wait_ge(st_expert, 32 * e)
                stage = prob[:, e % 2, :, :].rearrange("p h (c m) -> p (h c m)", c=1)
                hi = expert_hi[:, :, :].rearrange("p c d -> p (c d)")
                dve.tensor_copy(hi, stage).then_inc(expert_rounded, 1)
                dve.wait_ge(expert_rounded, e + 1)
                dve.tensor_tensor(expert_lo[:, :, :].rearrange("p c d -> p (c d)"), stage,
                                  hi.bitcast(F32), ALU.subtract).then_inc(expert_split, 1)
            dve.wait_ge(expert_split, E)
            dve.wait_ge(consts_set, HPC)
            dve.wait_ge(w_split, 4)
            dve.wait_ge(pool_ready, READY)
            dve.wait_ge(ld_const, 32)

            def slot(i, u, live):
                t = i * 4 + u
                pair, par = half(i, u), u // 2
                b4 = t - 4

                def bias(c):
                    if live(t):
                        wait(dve, scores_done, C * t + c + 1)
                        if c == 0:
                            wait(dve, ld_adj[par], 16 * (quarter(i, u) + 1))
                            wait(dve, turned, C * (t - 1))
                        dve.scalar_tensor_tensor(
                            out=prob[:, u % 2, HPC * c:HPC * (c + 1), :],
                            in0=ps_scores[c % 2][:, :].rearrange("p (h m) -> p h m", h=HPC),
                            scalar=HALF_SCALE,
                            in1=adj_in[:, par, u % 2, :].unsqueeze(1).to_broadcast([P, HPC, P]),
                            op0=ALU.mult, op1=ALU.add).then_inc(biased, 1)

                bias(0)
                bias(1)
                if live(b4):
                    wait(dve, y_rounded, b4 + 1)
                    wait(dve, stats_added, b4)
                    wide = ps_c[:, 0:(C - 1) * Y].rearrange("p (c n) -> p c n", c=C - 1)
                    dve.tensor_copy(sums[:, 0:C - 1, :], wide[:, :, P:Y])
                    dve.tensor_copy(sums[:, C - 1, :], ps_small[:, P:Y]).then_inc(sums_copied, 1)
                    dve.tensor_tensor(yT_lo[:, 0:C - 1, :], wide[:, :, 0:P],
                                      yT_hi[:, 0:C - 1, :].bitcast(F32), ALU.subtract)
                    dve.tensor_tensor(yT_lo[:, C - 1, :], ps_small[:, 0:P],
                                      yT_hi[:, C - 1, :].bitcast(F32), ALU.subtract).then_inc(y_split, 1)
                b = t - 1
                if live(b):
                    p2 = pv_mod(u, -1, 2)
                    wait(dve, exp_done, b + 1)
                    dve.reciprocal(inv_sum[:, :], row_sum[:, p2, :]).then_inc(sum_inverted, 1)
                    wait(dve, sum_inverted, b + 1)
                    dve.scalar_tensor_tensor(out=inv_nz[:, :], in0=abs_max[:, p2, :], scalar=0.0,
                                             in1=inv_sum[:, :], op0=ALU.not_equal,
                                             op1=ALU.mult).then_inc(zero_rows_out, 1)
                    wait(dve, zero_rows_out, b + 1)
                    dve.tensor_tensor(prob[:, p2, :, :], prob[:, p2, :, :],
                                      inv_nz[:, :].unsqueeze(2).to_broadcast([P, HEADS, P]),
                                      ALU.mult).then_inc(normalised, 1)
                bias(2)
                bias(3)
                b = b4
                if live(b):
                    wait(dve, router_done, b + 1)
                    dve.tensor_tensor(logits[:, :], ps_small[:, P + 2:P + 2 + E], rb[:, :],
                                      ALU.add).then_inc(logits_made, 1)
                    wait(dve, logits_made, b + 1)
                    dve.tensor_reduce(top[:, :], logits[:, :], AX.X, ALU.max).then_inc(top_found, 1)
                    wait(dve, top_found, b + 1)
                    dve.scalar_tensor_tensor(out=ranked[:, :], in0=logits[:, :], scalar=top[:, :],
                                             in1=rank[:, :], op0=ALU.is_ge,
                                             op1=ALU.mult).then_inc(ranked_made, 1)
                    wait(dve, ranked_made, b + 1)
                    dve.tensor_reduce(best[:, :], ranked[:, :], AX.X, ALU.max).then_inc(best_found, 1)
                    wait(dve, best_found, b + 1)
                    dve.tensor_scalar(neg_best[:, :], best[:, :], 1.0, -1.0, ALU.max,
                                      ALU.mult).then_inc(best_negated, 1)
                    dve.tensor_scalar(one_hot[:, :], ranked[:, :], best[:, :], None,
                                      ALU.is_equal).then_inc(hot_made, 1)
                    wait(dve, best_negated, b + 1)
                    dve.tensor_scalar(expert_of[:, bass.ds(b, 1)], neg_best[:, :], float(E), None,
                                      ALU.add).then_inc(expert_known, 1)
                if live(t):
                    wait(dve, biased, C * (t + 1))
                    dve.tensor_reduce(neg_max[:, u % 2, :], prob[:, u % 2, :, :], AX.X, ALU.max,
                                      negate=True).then_inc(max_found, 1)
                    wait(dve, max_found, t + 1)
                    dve.tensor_scalar(neg_max2[:, u % 2, :], neg_max[:, u % 2, :], 2.0, None,
                                      ALU.mult).then_inc(max_doubled, 1)
                    dve.tensor_reduce(abs_max[:, u % 2, :], prob[:, u % 2, :, :], AX.X, ALU.max,
                                      apply_absolute_value=True).then_inc(abs_found, 1)
                b = t + 1
                if live(b):
                    side, dpar = (u + 1) % 2, pv_mod(u, 1, 4) // 2
                    wait(dve, qk_copied, C * (half(i, u, 1) + 1))
                    wait(dve, scores_done, C * b)
                    for h in range(HPC):
                        last = dve.tensor_scalar(k_diag[:, :, h, :], qk[:, dpar, :, 1, side * P:side * P + P],
                                                 head_rows[:, h:h + 1], None, ALU.mult)
                    last.then_inc(diag_built, 1)
                if live(b4):
                    b = b4
                    wait(dve, hot_made, b + 1)
                    wait(dve, sums_copied, b + 1)
                    dve.tensor_tensor(count[:, :], count[:, :], one_hot[:, :], ALU.add)
                    dve.tensor_tensor(picked[:, :, :], one_hot[:, :].unsqueeze(2).to_broadcast([P, E, C]),
                                      sums[:, :, 0].unsqueeze(1).to_broadcast([P, E, C]),
                                      ALU.mult).then_inc(picked_made, 1)
                    wait(dve, picked_made, b + 1)
                    dve.tensor_tensor(conv_sum[:, :, :], conv_sum[:, :, :], picked[:, :, :],
                                      ALU.add).then_inc(stats_added, 1)
                b = t - 2
                if live(b):
                    p2 = u % 2
                    wait(dve, proj_done, b + 1)
                    wait(dve, ld_x[p2], 16 * (half(i, u, -2) + 1))
                    wait(dve, y_done, b - 1)
                    if not isinstance(t, int) or b // 2 > 0:
                        wait(dve, st_x1[p2], 16 * half(i, u, -2))
                    dve.tensor_tensor(x1[:, p2, :], ps_b[:, :], x_in[:, p2, :],
                                      ALU.add).then_inc(residual_added, 1)
                    wait(dve, residual_added, b + 1)
                    dve.bn_stats(stats[:, :], x1[:, p2, :]).then_inc(stats_taken, 1)
                    wait(dve, stats_taken, b + 1)
                b = t - 3
                if live(b):
                    p4 = pv_mod(u, -3, 4)
                    wait(dve, ld_adjT[p4 // 2], 16 * (quarter(i, u, -3) + 1))
                    dve.tensor_reduce(adjT_in[:, p4 // 2, p4 % 2, P:P + 1], adjT_in[:, p4 // 2, p4 % 2, 0:P],
                                      AX.X, ALU.add).then_inc(rows_summed, 1)
                if live(t - 2):
                    dve.bn_aggr(mean_var[:, :], stats[:, :]).then_inc(stats_joined, 1)
                    b = t - 2
                    wait(dve, stats_joined, b + 1)
                    dve.tensor_scalar(var_eps[:, :], mean_var[:, 1:2], EPS, None,
                                      ALU.add).then_inc(var_ready, 1)
                b = t - 1
                if live(b):
                    wait(dve, oT_rounded, b + 1)
                    wait(dve, proj_done, b)
                    dve.tensor_tensor(oT_lo[:, :, :].rearrange("p c n -> p (c n)"), ps_c[:, :],
                                      oT_hi[:, :, :].rearrange("p c n -> p (c n)").bitcast(F32),
                                      ALU.subtract).then_inc(oT_split, 1)
                b = t - 2
                if live(b):
                    wait(dve, rstd_made, b + 1)
                    dve.tensor_scalar(x1[:, u % 2, :], x1[:, u % 2, :], mean_var[:, 0:1], rstd[:, :],
                                      ALU.subtract, ALU.mult).then_inc(x1_ready, 1)

            run_slots(dve, slot, -2)

        phase_one.close()
        p1.close()
        phase_two(nc, ctx, locals())


def phase_two(nc, ctx, v):
    (B, D, E, C, N) = (v[k] for k in ("B", "D", "E", "C", "N"))
    out, x1_dram, conv_dram = v["out"], v["x1_dram"], v["conv_dram"]
    minus_half = v["minus_half"]
    ident = v["ident"]
    ones, expert_of = v["ones"], v["expert_of"]
    square_sum, conv_sum, count, bank = v["square_sum"], v["conv_sum"], v["count"], v["bank"]
    G = 4
    NG = B // G
    RING = 8 if NG % 8 == 0 and NG > 8 else 4
    assert NG % RING == 0 and NG > RING

    def sb(name, shape, dt=F32):
        return ctx.enter_context(nc.sbuf_tensor(name, shape, dt))

    def sem(name):
        return ctx.enter_context(nc.semaphore(name))

    experts = sb("experts", [P, E * C * D])
    bn_scale = sb("bn_scale", [P, E * D])
    bn_shift = sb("bn_shift", [P, E * D])
    gamma_t = sb("gamma_t", [P, E, C])
    beta_t = sb("beta_t", [P, E, C])
    mean_t = sb("mean_t", [P, E, C])
    mean_sq_t = sb("mean_sq_t", [P, E, C])
    var_t = sb("var_t", [P, E, C])
    inv_std_t = sb("inv_std_t", [P, E, C])
    scale_t = sb("scale_t", [P, E, C])
    shift_t = sb("shift_t", [P, E, C])
    nodes = sb("nodes", [P, E])
    inv_nodes = sb("inv_nodes", [P, E])
    conv_in = sb("conv_in", [P, RING, G, D])
    x1_in = sb("x1_in", [P, RING, G, D])
    stats = sb("stats2", [P, G, 6])
    mean_var = sb("mean_var2", [P, 2, G, 2])
    var_eps = sb("var_eps2", [P, 2, G])
    rstd = sb("rstd2", [P, 2, G])
    shift = sb("shift2", [P, 2, G])

    ld_bn = sem("ld_bn")
    ld_experts = sem("ld_experts")
    ld_g = [sem(f"ld_g{i}") for i in range(RING)]
    st_g = [sem(f"st_g{i}") for i in range(RING)]
    summed = sem("summed")
    var_known = sem("var_known")
    inverted = sem("inverted")
    table_step = sem("table_step")
    columns_ready = sem("columns_ready")
    spread = sem("spread")
    table_ready = sem("table_ready")
    dve_passed = sem("dve_passed")
    scaled = sem("scaled")
    shifted = sem("shifted")
    joined = sem("joined")
    stats_taken = sem("stats_taken2")
    stats_joined = sem("stats_joined2")
    var_ready = sem("var_ready2")
    rstd_made = sem("rstd_made2")
    shift_made = sem("shift_made2")
    finished = sem("finished")

    def run_groups(eng, group):
        for r in range(RING):
            group(0, r)
        with eng.Fori(1, NG // RING, 1) as k:
            for r in range(RING):
                group(k, r)

    block = ctx.enter_context(nc.Block())

    @block.sync
    def _(sp):
        sp.dma_start(experts[:, :], v["expert_w"]).then_inc(ld_experts, 16)
        sp.dma_start(gamma_t[:, :, :], v["gamma"]).then_inc(ld_bn, 16)
        sp.dma_start(beta_t[:, :, :], v["beta"]).then_inc(ld_bn, 16)

        def load(k, r):
            g = k * RING + r
            if not isinstance(k, int) or k > 0:
                sp.wait_ge(st_g[r], k * 16)
            sp.dma_start(conv_in[:, r, :, :], conv_dram[:, bass.ds(g * G, G), :]).then_inc(ld_g[r], 16)
            sp.dma_start(x1_in[:, r, :, :], x1_dram[:, bass.ds(g * G, G), :]).then_inc(ld_g[r], 16)

        run_groups(sp, load)

    @block.tensor
    def _(pe):
        for e in range(E):
            for j in range(C):
                pe.matmul(bank[0][:, e * C + j:e * C + j + 1],
                          square_sum[:, e * D + j * P:e * D + (j + 1) * P], ones[:, :], start=True, stop=True)
        pe.wait_ge(ld_experts, 16)
        for e in range(E):
            for j in range(C):
                for c in range(C):
                    row = (e * C + c) * D + j * P
                    last = pe.matmul(bank[1][:, e * C + j:e * C + j + 1], experts[:, row:row + P],
                                     conv_sum[:, e, c:c + 1], start=(c == 0), stop=(c == C - 1))
        last.then_inc(summed, 1)
        pe.wait_ge(columns_ready, 1)
        for table in range(2):
            for e in range(E):
                for j in range(C):
                    column = (scale_t, shift_t)[table][:, e, j:j + 1]
                    last = pe.matmul(bank[4 * table + e][:, j * P:(j + 1) * P],
                                     column.to_broadcast([P, P]), ident[:, :], start=True, stop=True)
                last.then_inc(spread, 1)

    @block.gpsimd
    def _(pool):
        pool.wait_ge(var_known, 1)
        pool.tensor_tensor(inv_std_t[:, :, :], var_t[:, :, :], minus_half[:, :].unsqueeze(2).to_broadcast(
            [P, E, C]), ALU.pow).then_inc(inverted, 1)
        pool.wait_ge(table_ready, 2 * E)

        def root(g, p2):
            pool.wait_ge(var_ready, g + 1)
            if not isinstance(g, int) or g > 1:
                pool.wait_ge(finished, g - 1)
            pool.tensor_tensor(rstd[:, p2, :], var_eps[:, p2, :], minus_half[:, :].to_broadcast([P, G]),
                               ALU.pow).then_inc(rstd_made, 1)

        def group(k, r):
            g = k * RING + r
            pool.wait_ge(ld_g[r], (k + 1) * 32)
            for j in range(G):
                e = pool.value_load(expert_of[0:1, bass.ds(g * G + j, 1)], min_val=0, max_val=E - 1)
                pool.tensor_tensor(conv_in[:, r, j, :], conv_in[:, r, j, :],
                                   bn_scale[:, bass.ds(e * D, D)], ALU.mult).then_inc(scaled, 1)
            if not isinstance(g, int) or g > 0:
                root(g - 1, (r - 1) % 2)

        run_groups(pool, group)
        root(NG - 1, (NG - 1) % 2)

    @block.scalar
    def _(act):
        for table in range(2):
            for e in range(E):
                act.wait_ge(spread, table * E + e + 1)
                act.activation((bn_scale, bn_shift)[table][:, e * D:(e + 1) * D], bank[4 * table + e][:, :],
                               ACT.Copy).then_inc(table_ready, 1)

        def group(k, r):
            g = k * RING + r
            act.wait_ge(shift_made, g + 1)
            for j in range(G):
                last = act.activation(x1_in[:, r, j, :], x1_in[:, r, j, :], ACT.Identity,
                                      bias=shift[:, r % 2, j:j + 1], scale=rstd[:, r % 2, j:j + 1])
            last.then_inc(finished, 1)
            act.wait_ge(finished, g + 1)
            act.dma_start(out[bass.ds(g * G, G), :, :].rearrange("b n d -> n b d"),
                          x1_in[:, r, :, :]).then_inc(st_g[r], 16)

        run_groups(act, group)
        for r in range(RING):
            act.wait_ge(st_g[r], 16 * (NG // RING))

    @block.vector
    def _(dve):
        steps = [0]

        def step(ins):
            steps[0] += 1
            ins.then_inc(table_step, 1)
            dve.wait_ge(table_step, steps[0])

        per_node = inv_nodes[:, :].unsqueeze(2).to_broadcast([P, E, C])
        step(dve.tensor_scalar(nodes[:, :], count[:, :], float(N), 1.0, ALU.mult, ALU.max))
        step(dve.reciprocal(inv_nodes[:, :], nodes[:, :]))
        dve.wait_ge(summed, 1)
        dve.wait_ge(ld_bn, 32)
        step(dve.tensor_tensor(mean_t[:, :, :], bank[1][:, 0:E * C].rearrange("p (e c) -> p e c", e=E),
                               per_node, ALU.mult))
        step(dve.tensor_tensor(mean_sq_t[:, :, :], mean_t[:, :, :], mean_t[:, :, :], ALU.mult))
        step(dve.tensor_tensor(var_t[:, :, :], bank[0][:, 0:E * C].rearrange("p (e c) -> p e c", e=E),
                               per_node, ALU.mult))
        step(dve.tensor_tensor(var_t[:, :, :], var_t[:, :, :], mean_sq_t[:, :, :], ALU.subtract))
        dve.tensor_scalar(var_t[:, :, :], var_t[:, :, :], EPS, None, ALU.add).then_inc(var_known, 1)
        dve.wait_ge(inverted, 1)
        step(dve.tensor_tensor(scale_t[:, :, :], gamma_t[:, :, :], inv_std_t[:, :, :], ALU.mult))
        step(dve.tensor_tensor(mean_t[:, :, :], mean_t[:, :, :], scale_t[:, :, :], ALU.mult))
        dve.tensor_tensor(shift_t[:, :, :], beta_t[:, :, :], mean_t[:, :, :],
                          ALU.subtract).then_inc(columns_ready, 1)
        dve.wait_ge(table_ready, 2 * E)

        def finish_stats(g, p2):
            dve.wait_ge(rstd_made, g + 1)
            if not isinstance(g, int) or g > 1:
                dve.wait_ge(finished, g - 1)
            dve.scalar_tensor_tensor(out=shift[:, p2, :], in0=mean_var[:, p2, :, 0], scalar=-1.0,
                                     in1=rstd[:, p2, :], op0=ALU.mult, op1=ALU.mult).then_inc(shift_made, 1)

        def group(k, r):
            g = k * RING + r
            for j in range(G):
                n = g * G + j
                e = dve.value_load(expert_of[0:1, bass.ds(n, 1)], min_val=0, max_val=E - 1)
                dve.wait_ge(scaled, n + 1)
                dve.tensor_tensor(conv_in[:, r, j, :], conv_in[:, r, j, :],
                                  bn_shift[:, bass.ds(e * D, D)], ALU.add).then_inc(shifted, 1)
            for j in range(G):
                dve.wait_ge(shifted, g * G + j + 1)
                dve.scalar_tensor_tensor(out=x1_in[:, r, j, :], in0=conv_in[:, r, j, :], scalar=0.0,
                                         in1=x1_in[:, r, j, :], op0=ALU.max,
                                         op1=ALU.add).then_inc(joined, 1)
            for j in range(G):
                dve.wait_ge(joined, g * G + j + 1)
                dve.bn_stats(stats[:, j, :], x1_in[:, r, j, :]).then_inc(stats_taken, 1)
            if not isinstance(g, int) or g > 0:
                finish_stats(g - 1, (r - 1) % 2)
            dve.wait_ge(stats_taken, (g + 1) * G)
            dve.sem_inc(dve_passed)
            for j in range(G):
                dve.bn_aggr(mean_var[:, r % 2, j, :], stats[:, j, :]).then_inc(stats_joined, 1)
            dve.wait_ge(stats_joined, (g + 1) * G)
            dve.tensor_scalar(var_eps[:, r % 2, :], mean_var[:, r % 2, :, 1], EPS, None,
                              ALU.add).then_inc(var_ready, 1)

        run_groups(dve, group)
        finish_stats(NG - 1, (NG - 1) % 2)


def kernel(x, adj, L0_gnn_Wq, L0_gnn_Wk, L0_gnn_Wv, L0_gnn_Wo, L1_gnn_router_w, L1_gnn_router_b,
           L1_gnn_expert_w, L1_gnn_bn_gamma, L1_gnn_bn_beta):
    import numpy as np
    import concourse.bacc as bacc
    from concourse.bass_utils import run_bass_kernel_spmd

    x, adj = np.asarray(x), np.asarray(adj)
    B, N, D = x.shape
    E = L1_gnn_bn_gamma.shape[0]
    C = D // P

    def weight(w):
        w = np.asarray(w).T.reshape(C, P, D)
        return w.transpose(1, 0, 2).reshape(P, C * D)

    arrays = {
        "x": x,
        "xT": x.reshape(B // 2, 2 * N, C, P).transpose(3, 0, 2, 1).reshape(P, B // 2, C * 2 * N),
        "adj": adj,
        "adjT": adj.transpose(2, 0, 1),
        "wqT": weight(L0_gnn_Wq), "wkT": weight(L0_gnn_Wk),
        "wvT": weight(L0_gnn_Wv), "woT": weight(L0_gnn_Wo),
        "router_w": np.asarray(L1_gnn_router_w).reshape(C, P, E).transpose(1, 0, 2),
        "router_b": np.asarray(L1_gnn_router_b),
        "expert_w": np.asarray(L1_gnn_expert_w).reshape(E, C, P, D).transpose(2, 0, 1, 3).reshape(P, E * C * D),
        "gamma": np.asarray(L1_gnn_bn_gamma).reshape(E, C, P).transpose(2, 0, 1),
        "beta": np.asarray(L1_gnn_bn_beta).reshape(E, C, P).transpose(2, 0, 1),
    }
    arrays = {k: np.ascontiguousarray(a) for k, a in arrays.items()}
    nc = bacc.Bacc("TRN2", target_bir_lowering=False, num_devices=1)
    ins = [nc.dram_tensor(k, a.shape, F32, kind="ExternalInput").ap() for k, a in arrays.items()]
    out = nc.dram_tensor("out", (B, N, D), F32, kind="ExternalOutput").ap()
    graph_block_program(nc, *ins, out)
    r = run_bass_kernel_spmd(nc, [arrays], core_ids=[0])
    return r.results[0]["out"]
```

```python
from contextlib import ExitStack

import concourse.bass as bass
from concourse import mybir
from concourse.alu_op_type import AluOpType as ALU

F32 = mybir.dt.float32
F32R = mybir.dt.float32r
I32 = mybir.dt.int32
ACT = mybir.ActivationFunctionType
AX = mybir.AxisListType

P = 128
HEADS = 16
EPS = 1e-5


def graph_block_program(nc, x, xT, adj, adjT, wqT, wkT, wvT, woT, router_w, router_b, expert_w,
                        gamma, beta, out):
    B, N, D = x.shape
    E = router_w.shape[2]
    C = D // P
    HPC = HEADS // C
    HD = D // HEADS
    HALF_SCALE = 0.5 * float(D) ** -0.5
    assert N == P and HD == 32 and B % 4 == 0 and B >= 20

    x1_dram = nc.dram_tensor("x1_scratch", (P, B, D), F32, kind="Internal").ap()
    expert_hi_dram = nc.dram_tensor("expert_hi_scratch", (E, P, C, D), F32, kind="Internal").ap()
    expert_lo_dram = nc.dram_tensor("expert_lo_scratch", (E, P, C, D), F32, kind="Internal").ap()
    conv_dram = nc.dram_tensor("conv_scratch", (P, B, D), F32, kind="Internal").ap()

    with ExitStack() as ctx:
        def sem(name):
            return ctx.enter_context(nc.semaphore(name))

        expert_of = ctx.enter_context(nc.sbuf_tensor("expert_of", [1, B], I32))
        square_sum = ctx.enter_context(nc.sbuf_tensor("square_sum", [P, E * D], F32))
        conv_sum = ctx.enter_context(nc.sbuf_tensor("conv_sum", [P, E * C], F32))
        ident = ctx.enter_context(nc.sbuf_tensor("ident", [P, P], F32))
        constants = ctx.enter_context(nc.sbuf_tensor("constants", [P, 2], F32))
        ones, minus_half = constants[:, 0:1], constants[:, 1:2]
        bank = [ctx.enter_context(nc.psum_tensor(f"bank{i}", [P, 512], F32)) for i in range(8)]
        ps_scores, ps_turned = bank[0:2], bank[2:4]
        ps_a, ps_b, ps_c, ps_small = bank[4:8]

        p1 = ExitStack()

        def sb(name, shape, dt=F32):
            return p1.enter_context(nc.sbuf_tensor(name, shape, dt))

        w_hi = {k: sb(f"w{k}_hi", [P, C, D], F32R) for k in "qkvo"}
        w_lo = {k: sb(f"w{k}_lo", [P, C, D], F32R) for k in "qkvo"}
        xT_in = sb("xT_in", [P, C, 2 * P])
        xT_hi = sb("xT_hi", [P, 2, C, 2 * P], F32R)
        xT_lo = sb("xT_lo", [P, 2, C, 2 * P], F32R)
        x_in = sb("x_in", [P, 2, D])
        adj_in = sb("adj_in", [P, 2, 2, P])
        adjT_in = sb("adjT_in", [P, 2, 2, P + 2])
        qk = sb("qk", [P, 2, C, 2, 2 * P])
        v = sb("v", [P, 4, D])
        q_hi = sb("q_hi", [P, C, P], F32R)
        q_lo = sb("q_lo", [P, C, P], F32R)
        k_hi = sb("k_hi", [P, C, HPC, P], F32R)
        k_lo = sb("k_lo", [P, C, HPC, P], F32R)
        prob = sb("prob", [P, 2, HEADS, P])
        probT = sb("probT", [P, HEADS, P])
        oT_hi = sb("oT_hi", [P, C, P], F32R)
        oT_lo = sb("oT_lo", [P, C, P], F32R)
        x1 = sb("x1", [P, 2, D])
        yT_hi = sb("yT_hi", [P, 2, C, P], F32R)
        yT_lo = sb("yT_lo", [P, 2, C, P], F32R)
        expert_hi = sb("expert_hi", [P, C, D], F32R)
        expert_lo = sb("expert_lo", [P, C, D], F32R)
        conv = sb("conv", [P, 2, D])
        square = sb("square", [P, D])
        head_rows = sb("head_rows", [P, HPC])
        rw = sb("rw", [P, C, E])
        neg_max2 = sb("neg_max2", [P, 2, HEADS])
        abs_max = sb("abs_max", [P, 2, HEADS])
        row_sum = sb("row_sum", [P, 2, HEADS])
        inv_sum = sb("inv_sum", [P, HEADS])
        norm = sb("norm", [P, 10])
        stats, mean_var, var_eps, rstd = norm[:, 0:6], norm[:, 6:8], norm[:, 8:9], norm[:, 9:10]
        sums = sb("sums", [P, C, 2])
        router = sb("router", [1, 4 * E + 3])
        rb, logits, ranked, rank = (router[:, i * E:(i + 1) * E] for i in range(4))
        top, best, neg_best = (router[:, i:i + 1] for i in range(4 * E, 4 * E + 3))

        ld_w = [sem(f"ld_w{i}") for i in range(4)]
        ld_const = sem("ld_const")
        ld_expert = sem("ld_expert")
        squares_cleared = sem("squares_cleared")
        st_expert = sem("st_expert")
        ld_hi = sem("ld_hi")
        ld_lo = sem("ld_lo")
        ld_xT = sem("ld_xT")
        ld_x = [sem("ld_x0"), sem("ld_x1")]
        ld_adj = [sem("ld_adj0"), sem("ld_adj1")]
        ld_adjT = [sem("ld_adjT0"), sem("ld_adjT1")]
        st_x1 = [sem("st_x1_0"), sem("st_x1_1")]
        st_conv = [sem("st_conv0"), sem("st_conv1")]
        pool_zeroed = sem("pool_zeroed")
        pool_ready = sem("pool_ready")
        pool_passed = sem("pool_passed")
        x_split = sem("x_split")
        x_rounded = sem("x_rounded")
        squares_added = sem("squares_added")
        rstd_made = sem("rstd_made")
        scores_done = sem("scores_done")
        qk_done = sem("qk_done")
        v_done = sem("v_done")
        turned = sem("turned")
        pv_done = sem("pv_done")
        proj_done = sem("proj_done")
        y_done = sem("y_done")
        router_done = sem("router_done")
        conv_done = sem("conv_done")
        qk_copied = sem("qk_copied")
        v_copied = sem("v_copied")
        probT_copied = sem("probT_copied")
        exp_done = sem("exp_done")
        qk_rounded = sem("qk_rounded")
        oT_rounded = sem("oT_rounded")
        y_rounded = sem("y_rounded")
        conv_copied = sem("conv_copied")
        squared = sem("squared")
        w_rounded = sem("w_rounded")
        w_split = sem("w_split")
        rows_cleared = sem("rows_cleared")
        consts_set = sem("consts_set")
        qk_split = sem("qk_split")
        biased = sem("biased")
        max_found = sem("max_found")
        max_doubled = sem("max_doubled")
        abs_found = sem("abs_found")
        sum_inverted = sem("sum_inverted")
        zero_rows_out = sem("zero_rows_out")
        normalised = sem("normalised")
        oT_split = sem("oT_split")
        residual_added = sem("residual_added")
        stats_taken = sem("stats_taken")
        stats_joined = sem("stats_joined")
        var_ready = sem("var_ready")
        x1_ready = sem("x1_ready")
        rows_summed = sem("rows_summed")
        sums_copied = sem("sums_copied")
        y_split = sem("y_split")
        expert_rounded = sem("expert_rounded")
        expert_split = sem("expert_split")
        logits_made = sem("logits_made")
        top_found = sem("top_found")
        ranked_made = sem("ranked_made")
        best_found = sem("best_found")
        best_negated = sem("best_negated")
        expert_known = sem("expert_known")
        stats_added = sem("stats_added")

        SLOT_LOOP_START, SLOT_LOOP_END, SLOT_END = 8, B - 8, B + 6

        def run_slots(eng, slot, first):
            for t in range(first, SLOT_LOOP_START):
                slot(t // 4, t % 4, lambda b: 0 <= b < B)
            with eng.Fori(SLOT_LOOP_START // 4, SLOT_LOOP_END // 4, 1) as i:
                for u in range(4):
                    slot(i, u, lambda b: True)
            for t in range(SLOT_LOOP_END, SLOT_END):
                slot(t // 4, t % 4, lambda b: 0 <= b < B)

        def wait(eng, s, value):
            if not isinstance(value, int) or value > 0:
                eng.wait_ge(s, value)

        def half(i, u, k=0):
            return i * 2 + (u + k) // 2

        def quarter(i, u, k=0):
            return i + (u + k) // 4

        def pv_mod(u, k, m):
            return (u + k) % m

        Y = P + 2
        READY = 5 + E

        phase_one = ExitStack()
        block = phase_one.enter_context(nc.Block())

        @block.sync
        def _(sp):
            def load_xT(pair):
                wait(sp, x_split, pair)
                sp.dma_start(xT_in[:, :, :], xT[:, bass.ds(pair, 1), :].rearrange(
                    "p g (c n) -> p (g c) n", c=C)).then_inc(ld_xT, 16)

            for i, (k, w) in enumerate(zip("vqko", (wvT, wqT, wkT, woT))):
                if i == 1:
                    load_xT(0)
                if i >= 2:
                    sp.wait_ge(w_split, i - 1)
                sp.dma_start(prob[:, i % 2, :, :].rearrange("p h m -> p (h m)"),
                             w).then_inc(ld_w[i], 16)
            for dst, src in ((rw[:, :, :], router_w), (rb[:, :], router_b.unsqueeze(0))):
                sp.dma_start(dst, src).then_inc(ld_const, 16)
            def slot(i, u, live):
                t = i * 4 + u
                b = t - 3
                if live(b):
                    wait(sp, x1_ready, b + 1)
                    par = pv_mod(u, -3, 2)
                    sp.dma_start(x1_dram[:, bass.ds(b, 1), :].rearrange("p b d -> p (b d)"),
                                 x1[:, par, :]).then_inc(st_x1[par], 16)
                b = t - 6
                if live(b):
                    wait(sp, conv_copied, b + 1)
                    par = pv_mod(u, -6, 2)
                    sp.dma_start(conv_dram[:, bass.ds(b, 1), :].rearrange("p b d -> p (b d)"),
                                 conv[:, par, :]).then_inc(st_conv[par], 16)
                if u % 2 == 0:
                    g = half(i, u)
                    pair = g + 1
                    if live(2 * pair):
                        par = (u // 2 + 1) % 2
                        wait(sp, biased, 8 * g)
                        sp.dma_start(adj_in[:, par, :, :], adj[bass.ds(2 * pair, 2), :, :].rearrange(
                            "b n m -> n b m")).then_inc(ld_adj[par], 16)
                    pair = g - 1
                    if live(2 * pair):
                        par = (u // 2 + 1) % 2
                        wait(sp, y_done, 2 * g - 4)
                        sp.dma_start(adjT_in[:, par, :, 0:P], adjT[:, bass.ds(2 * pair, 2), :]
                                     ).then_inc(ld_adjT[par], 16)
                b = t - 4
                if live(b):
                    wait(sp, expert_known, b + 1)
                    e = sp.value_load(expert_of[0:1, bass.ds(b, 1)], min_val=0, max_val=E - 1)
                    if isinstance(b, int) and b == 0:
                        sp.wait_ge(st_expert, 32 * E)
                    wait(sp, conv_done, b)
                    sp.dma_start(expert_hi[:, :, :].bitcast(F32), expert_hi_dram[bass.ds(e, 1), :, :, :].rearrange(
                        "e p c d -> p (e c) d")).then_inc(ld_hi, 16)
                    sp.dma_start(expert_lo[:, :, :].bitcast(F32), expert_lo_dram[bass.ds(e, 1), :, :, :].rearrange(
                        "e p c d -> p (e c) d")).then_inc(ld_lo, 16)
                if live(t):
                    wait(sp, residual_added, t - 1)
                    sp.dma_start(x_in[:, u % 2, :], x[bass.ds(t, 1), :, :].rearrange(
                        "b n d -> n (b d)")).then_inc(ld_x[u % 2], 16)
                if u % 2 == 0:
                    g = half(i, u)
                    if live(2 * (g + 3)) and (not isinstance(t, int) or g + 3 > 0):
                        load_xT(g + 3)
                if isinstance(t, int) and -2 <= t <= E - 2:
                    e = t + 2
                    if e >= 1:
                        sp.wait_ge(expert_split, e)
                        sp.dma_start(expert_hi_dram[e - 1, :, :, :],
                                     expert_hi[:, :, :].bitcast(F32)).then_inc(st_expert, 16)
                        sp.dma_start(expert_lo_dram[e - 1, :, :, :],
                                     expert_lo[:, :, :].bitcast(F32)).then_inc(st_expert, 16)
                    if e < E:
                        sp.dma_start(square_sum[:, :], expert_w[:, e * C * D:(e + 1) * C * D]
                                     ).then_inc(ld_expert, 16)

            run_slots(sp, slot, -4)
            for par in range(2):
                sp.wait_ge(st_x1[par], 16 * (B // 2))
                sp.wait_ge(st_conv[par], 16 * (B // 2))

        @block.gpsimd
        def _(pool):
            pool.memset(ident[:, :], 0.0).then_inc(pool_zeroed, 1)
            pool.memset(conv_sum[:, :], 0.0).then_inc(pool_ready, 1)
            pool.memset(adjT_in[:, :, :, P + 1:P + 2], 1.0 / N).then_inc(pool_ready, 1)
            pool.memset(ones[:, :], 1.0).then_inc(pool_ready, 1)
            pool.memset(minus_half[:, :], -0.5).then_inc(pool_ready, 1)
            for e in range(E):
                pool.memset(rank[:, e:e + 1], float(E - e)).then_inc(pool_ready, 1)
            pool.wait_ge(pool_zeroed, 1)
            pool.affine_select(out=ident[:, :], in_=ident[:, :], compare_op=ALU.not_equal, fill=1.0,
                               base=0, pattern=[[-1, P]], channel_multiplier=1).then_inc(pool_ready, 1)
            pool.wait_ge(pool_ready, READY - 1)

            def split_xT(pair, par):
                wait(pool, ld_xT, 16 * (pair + 1))
                wait(pool, v_done, 2 * pair - 2)
                wait(pool, qk_done, C * (pair - 1))
                pool.sem_inc(pool_passed)
                pool.tensor_copy(xT_hi[:, par, :, :], xT_in[:, :, :]).then_inc(x_rounded, 1)
                wait(pool, x_rounded, pair + 1)
                pool.tensor_tensor(xT_lo[:, par, :, :], xT_in[:, :, :],
                                   xT_hi[:, par, :, :].bitcast(F32), ALU.subtract).then_inc(x_split, 1)

            def slot(i, u, live):
                t = i * 4 + u
                if u % 2 == 0:
                    pair = half(i, u) + 2
                    if live(2 * pair):
                        split_xT(pair, (u // 2) % 2)
                if live(t - 2):
                    wait(pool, var_ready, t - 1)
                    pool.tensor_tensor(rstd[:, :], var_eps[:, :], minus_half[:, 0:1],
                                       ALU.pow).then_inc(rstd_made, 1)
                b = t - 4
                if live(b):
                    wait(pool, expert_known, b + 1)
                    e = pool.value_load(expert_of[0:1, bass.ds(b, 1)], min_val=0, max_val=E - 1)
                    wait(pool, stats_added, b)
                    acc = conv_sum[:, bass.ds(e * C, C)]
                    pool.tensor_tensor(acc, acc, sums[:, :, 0], ALU.add).then_inc(stats_added, 1)
                b = t - 5
                if live(b):
                    if isinstance(b, int) and b == 0:
                        pool.wait_ge(squares_cleared, 1)
                    e = pool.value_load(expert_of[0:1, bass.ds(b, 1)], min_val=0, max_val=E - 1)
                    wait(pool, squared, b + 1)
                    wait(pool, squares_added, b)
                    acc = square_sum[:, bass.ds(e * D, D)]
                    pool.tensor_tensor(acc, acc, square[:, :], ALU.add).then_inc(squares_added, 1)

            run_slots(pool, slot, -4)

        @block.tensor
        def _(pe):
            def mm(dst, lhsT, rhs, start, stop):
                return pe.matmul(dst, lhsT, rhs, start=start, stop=stop)

            def mm3(dst, lhs, rhs):
                n = len(lhs)
                for i, ((lh, ll), (rh, rl)) in enumerate(zip(lhs, rhs)):
                    mm(dst, lh, rh, i == 0, False)
                    mm(dst, lh, rl, False, False)
                    last = mm(dst, ll, rh, False, i == n - 1)
                return last

            pe.wait_ge(pool_ready, READY)
            pe.wait_ge(w_split, 3)

            def slot(i, u, live):
                t = i * 4 + u
                pair = half(i, u)
                par = u // 2

                def scores(c):
                    b = t
                    if not live(b):
                        return
                    if c == 0:
                        wait(pe, qk_split, b + 1)
                    wait(pe, biased, C * b + c - 1)
                    mm3(ps_scores[c % 2][:, :], [(q_hi[:, c, :], q_lo[:, c, :])],
                        [(k_hi[:, c, :, :].rearrange("p h m -> p (h m)"),
                          k_lo[:, c, :, :].rearrange("p h m -> p (h m)"))]).then_inc(scores_done, 1)

                def project_qk(c, dst):
                    nxt, npar = pair + 1, (par + 1) % 2
                    if not live(2 * nxt):
                        return
                    wait(pe, x_split, nxt + 1)
                    for i, k in enumerate("qk"):
                        last = mm3(dst[:, i * 2 * P:(i + 1) * 2 * P],
                                   [(w_hi[k][:, j, c * P:(c + 1) * P], w_lo[k][:, j, c * P:(c + 1) * P])
                                    for j in range(C)],
                                   [(xT_hi[:, npar, j, :], xT_lo[:, npar, j, :]) for j in range(C)])
                    last.then_inc(qk_done, 1)

                def turn(c):
                    b = t - 1
                    if not live(b):
                        return
                    if c == 0:
                        wait(pe, normalised, b + 1)
                    wait(pe, probT_copied, C * b + c - 1)
                    for h in range(HPC):
                        last = pe.transpose(ps_turned[c % 2][:, h * P:(h + 1) * P],
                                            prob[:, pv_mod(u, -1, 2), HPC * c + h, :], ident[:, :])
                    last.then_inc(turned, 1)

                def times_v(c):
                    b = t - 1
                    if not live(b):
                        return
                    if c == 0:
                        wait(pe, v_copied, b + 1)
                        wait(pe, y_split, b - 2)
                    wait(pe, probT_copied, C * b + c + 1)
                    for h in range(HPC):
                        col = (HPC * c + h) * HD
                        last = mm(ps_c[HD * h:HD * h + HD, c * P:(c + 1) * P],
                                  v[:, pv_mod(u, -1, 4), col:col + HD], probT[:, HPC * c + h, :], True, True)
                    if c == C - 1:
                        last.then_inc(pv_done, 1)

                scores(0)
                scores(1)
                b6 = t - 6
                if live(2 * (pair + 1)):
                    if live(b6):
                        wait(pe, squared, b6 + 1)
                    else:
                        wait(pe, v_copied, t + 2)
                project_qk((2 * u) % C, ps_a)
                scores(2)
                scores(3)
                if live(2 * (pair + 1)):
                    if live(t - 3):
                        wait(pe, residual_added, t - 2)
                    else:
                        wait(pe, qk_copied, C * (pair + 1) + (2 * u) % C)
                project_qk((2 * u) % C + 1, ps_b)
                turn(0)
                turn(1)
                b = t - 4
                if live(b):
                    if isinstance(b, int) and b == 0:
                        pe.wait_ge(ld_const, 32)
                    wait(pe, y_split, b + 1)
                    for c in range(C):
                        last = mm(ps_small[0:1, P + 2:P + 2 + E], sums[:, c, 1:2],
                                  rw[:, c, :], c == 0, c == C - 1)
                    last.then_inc(router_done, 1)
                b = t + 2
                if live(b):
                    nxt, npar = pair + 1, (par + 1) % 2
                    wait(pe, qk_copied, C * nxt + (2 * u) % C + 1)
                    mm3(ps_a[:, :],
                        [(xT_hi[:, npar, j, u % 2 * P:u % 2 * P + P], xT_lo[:, npar, j, u % 2 * P:u % 2 * P + P])
                         for j in range(C)],
                        [(w_hi["v"][:, j, :], w_lo["v"][:, j, :]) for j in range(C)]).then_inc(v_done, 1)
                turn(2)
                turn(3)
                times_v(0)
                times_v(1)
                b = t - 2
                if live(b):
                    wait(pe, oT_split, b + 1)
                    if isinstance(b, int) and b == 0:
                        pe.wait_ge(w_split, 4)
                    if live(2 * (pair + 1)):
                        wait(pe, qk_copied, C * (pair + 1) + (2 * u) % C + 2)
                    else:
                        wait(pe, residual_added, b)
                    mm3(ps_b[:, :], [(oT_hi[:, j, :], oT_lo[:, j, :]) for j in range(C)],
                        [(w_hi["o"][:, j, :], w_lo["o"][:, j, :]) for j in range(C)]).then_inc(proj_done, 1)
                times_v(2)
                times_v(3)
                b, y2 = t - 5, pv_mod(u, -5, 2)
                if live(b):
                    if live(t + 2):
                        wait(pe, v_copied, t + 3)
                    else:
                        wait(pe, squared, b)
                    wait(pe, ld_hi, (b + 1) * 16)
                    for c in range(C):
                        mm(ps_a[:, :], yT_hi[:, y2, c, :], expert_hi[:, c, :], c == 0, False)
                        mm(ps_a[:, :], yT_lo[:, y2, c, :], expert_hi[:, c, :], False, False)
                    wait(pe, ld_lo, (b + 1) * 16)
                    for c in range(C):
                        last = mm(ps_a[:, :], yT_hi[:, y2, c, :], expert_lo[:, c, :], False, c == C - 1)
                    last.then_inc(conv_done, 1)
                b = t - 3
                if live(b):
                    p4 = pv_mod(u, -3, 4)
                    wait(pe, x1_ready, b + 1)
                    wait(pe, rows_summed, b + 1)
                    if live(t - 1):
                        wait(pe, oT_split, t)
                    else:
                        wait(pe, y_split, b)
                    wait(pe, expert_known, b)
                    for c in range(C):
                        lhsT = x1[:, p4 % 2, c * P:(c + 1) * P]
                        dst = ps_c[:, c * Y:(c + 1) * Y] if c < C - 1 else ps_small[:, 0:Y]
                        last = mm(dst, lhsT, adjT_in[:, p4 // 2, p4 % 2, :], True, True)
                    last.then_inc(y_done, 1)

            run_slots(pe, slot, -2)

        @block.scalar
        def _(act):
            act.wait_ge(consts_set, HPC)
            def slot(i, u, live):
                t = i * 4 + u
                pair, par = half(i, u), u // 2
                nxt, npar = pair + 1, (par + 1) % 2
                b = t - 4
                if live(b):
                    wait(act, y_done, b + 1)
                    wait(act, conv_done, b - 1)
                    act.activation(yT_hi[:, u % 2, 0:C - 1, :], ps_c[:, 0:(C - 1) * Y].rearrange(
                        "p (c n) -> p c n", c=C - 1)[:, :, 0:P], ACT.Copy)
                    act.activation(yT_hi[:, u % 2, C - 1, :], ps_small[:, 0:P], ACT.Copy).then_inc(y_rounded, 1)

                def copy_qk(c, src):
                    if live(2 * nxt):
                        wait(act, qk_done, C * nxt + c + 1)
                        wait(act, scores_done, 2 * C * (nxt - 1))
                        act.activation(qk[:, npar, c, :, :].rearrange("p k n -> p (k n)"), src[:, :],
                                       ACT.Copy).then_inc(qk_copied, 1)

                def copy_turned(c):
                    if live(t - 1):
                        wait(act, turned, C * (t - 1) + c + 1)
                        wait(act, pv_done, t - 1)
                        act.activation(probT[:, HPC * c:HPC * (c + 1), :].rearrange("p h n -> p (h n)"),
                                       ps_turned[c % 2][:, :], ACT.Copy).then_inc(probT_copied, 1)

                copy_qk((2 * u) % C, ps_a)
                copy_qk((2 * u) % C + 1, ps_b)
                copy_turned(0)
                copy_turned(1)
                b = t + 1
                if live(b):
                    side, dpar = (u + 1) % 2, pv_mod(u, 1, 4) // 2
                    wait(act, qk_copied, C * (half(i, u, 1) + 1))
                    wait(act, scores_done, C * b)
                    act.activation(q_hi[:, :, :], qk[:, dpar, :, 0, side * P:side * P + P], ACT.Copy)
                    for h in range(HPC):
                        last = act.activation(k_hi[:, :, h, :], qk[:, dpar, :, 1, side * P:side * P + P],
                                              ACT.Copy, scale=head_rows[:, h:h + 1])
                    last.then_inc(qk_rounded, 1)
                if live(t + 2):
                    wait(act, v_done, t + 3)
                    wait(act, pv_done, t - 1)
                    act.activation(v[:, pv_mod(u, 2, 4), :], ps_a[:, :], ACT.Copy).then_inc(v_copied, 1)
                copy_turned(2)
                copy_turned(3)

                def exps(h0, h1):
                    if live(t):
                        for h in range(h0, h1):
                            last = act.activation(prob[:, u % 2, h, :], prob[:, u % 2, h, :], ACT.Exp,
                                                  bias=neg_max2[:, u % 2, h:h + 1], scale=2.0,
                                                  accum_out=row_sum[:, u % 2, h:h + 1])
                        if h1 == HEADS:
                            last.then_inc(exp_done, 1)

                if live(t):
                    wait(act, abs_found, t + 1)
                    wait(act, max_doubled, t + 1)
                exps(0, 6)
                b = t - 1
                if live(b):
                    wait(act, pv_done, b + 1)
                    wait(act, proj_done, b)
                    act.activation(oT_hi[:, :, :].rearrange("p c n -> p (c n)"), ps_c[:, :],
                                   ACT.Copy).then_inc(oT_rounded, 1)
                exps(6, 12)
                b = t - 5
                if live(b):
                    p2 = (u + 1) % 2
                    wait(act, conv_done, b + 1)
                    if not isinstance(t, int) or b // 2 > 0:
                        wait(act, st_conv[p2], 16 * half(i, u, -5))
                    act.activation(conv[:, p2, :], ps_a[:, :], ACT.Copy).then_inc(conv_copied, 1)
                    wait(act, squares_added, b)
                    act.activation(square[:, :], ps_a[:, :], ACT.Square).then_inc(squared, 1)
                exps(12, HEADS)

            run_slots(act, slot, -2)

        @block.vector
        def _(dve):
            dve.memset(head_rows[:, :], 0.0).then_inc(rows_cleared, 1)
            dve.wait_ge(rows_cleared, 1)
            for h in range(HPC):
                dve.memset(head_rows[HD * h:HD * h + HD, h:h + 1], 1.0).then_inc(consts_set, 1)
            for i, k in enumerate("vqko"):
                dve.wait_ge(ld_w[i], 16)
                stage = prob[:, i % 2, :, :].rearrange("p h m -> p (h m)")
                hi = w_hi[k][:, :, :].rearrange("p c d -> p (c d)")
                dve.tensor_copy(hi, stage).then_inc(w_rounded, 1)
                dve.wait_ge(w_rounded, i + 1)
                dve.tensor_tensor(w_lo[k][:, :, :].rearrange("p c d -> p (c d)"), stage,
                                  hi.bitcast(F32), ALU.subtract).then_inc(w_split, 1)
            dve.wait_ge(consts_set, HPC)
            dve.wait_ge(w_split, 4)
            dve.wait_ge(pool_ready, READY)
            dve.wait_ge(ld_const, 32)

            def split_expert(e):
                dve.wait_ge(ld_expert, 16 * (e + 1))
                if e:
                    dve.wait_ge(st_expert, 32 * e)
                hi = expert_hi[:, :, :].rearrange("p c d -> p (c d)")
                dve.tensor_copy(hi, square_sum[:, :]).then_inc(expert_rounded, 1)
                dve.wait_ge(expert_rounded, e + 1)
                dve.tensor_tensor(expert_lo[:, :, :].rearrange("p c d -> p (c d)"), square_sum[:, :],
                                  hi.bitcast(F32), ALU.subtract).then_inc(expert_split, 1)
                if e == E - 1:
                    dve.wait_ge(expert_split, E)
                    dve.memset(square_sum[:, :], 0.0).then_inc(squares_cleared, 1)

            def slot(i, u, live):
                t = i * 4 + u
                pair, par = half(i, u), u // 2
                b4 = t - 4

                def bias(c):
                    if live(t):
                        wait(dve, scores_done, C * t + c + 1)
                        if c == 0:
                            wait(dve, ld_adj[par], 16 * (quarter(i, u) + 1))
                            wait(dve, turned, C * (t - 1))
                        dve.scalar_tensor_tensor(
                            out=prob[:, u % 2, HPC * c:HPC * (c + 1), :],
                            in0=ps_scores[c % 2][:, :].rearrange("p (h m) -> p h m", h=HPC),
                            scalar=HALF_SCALE,
                            in1=adj_in[:, par, u % 2, :].unsqueeze(1).to_broadcast([P, HPC, P]),
                            op0=ALU.mult, op1=ALU.add).then_inc(biased, 1)

                bias(0)
                bias(1)
                b = t - 1
                if live(b):
                    p2 = pv_mod(u, -1, 2)
                    wait(dve, exp_done, b + 1)
                    dve.reciprocal(inv_sum[:, :], row_sum[:, p2, :]).then_inc(sum_inverted, 1)
                    wait(dve, sum_inverted, b + 1)
                    dve.scalar_tensor_tensor(out=inv_sum[:, :], in0=abs_max[:, p2, :], scalar=0.0,
                                             in1=inv_sum[:, :], op0=ALU.not_equal,
                                             op1=ALU.mult).then_inc(zero_rows_out, 1)
                    wait(dve, zero_rows_out, b + 1)
                    dve.tensor_tensor(prob[:, p2, :, :], prob[:, p2, :, :],
                                      inv_sum[:, :].unsqueeze(2).to_broadcast([P, HEADS, P]),
                                      ALU.mult).then_inc(normalised, 1)
                if live(b4):
                    wait(dve, y_rounded, b4 + 1)
                    wait(dve, stats_added, b4)
                    wide = ps_c[:, 0:(C - 1) * Y].rearrange("p (c n) -> p c n", c=C - 1)
                    dve.tensor_copy(sums[:, 0:C - 1, :], wide[:, :, P:Y])
                    dve.tensor_copy(sums[:, C - 1, :], ps_small[:, P:Y]).then_inc(sums_copied, 1)
                    dve.tensor_tensor(yT_lo[:, u % 2, 0:C - 1, :], wide[:, :, 0:P],
                                      yT_hi[:, u % 2, 0:C - 1, :].bitcast(F32), ALU.subtract)
                    dve.tensor_tensor(yT_lo[:, u % 2, C - 1, :], ps_small[:, 0:P],
                                      yT_hi[:, u % 2, C - 1, :].bitcast(F32), ALU.subtract).then_inc(y_split, 1)
                bias(2)
                bias(3)
                if live(t):
                    wait(dve, biased, C * (t + 1))
                    dve.tensor_reduce(neg_max2[:, u % 2, :], prob[:, u % 2, :, :], AX.X, ALU.max,
                                      negate=True).then_inc(max_found, 1)
                    wait(dve, max_found, t + 1)
                    dve.tensor_scalar(neg_max2[:, u % 2, :], neg_max2[:, u % 2, :], 2.0, None,
                                      ALU.mult).then_inc(max_doubled, 1)
                b = b4
                if live(b):
                    wait(dve, router_done, b + 1)
                    dve.tensor_tensor(logits[:, :], ps_small[0:1, P + 2:P + 2 + E], rb[:, :],
                                      ALU.add).then_inc(logits_made, 1)
                    wait(dve, logits_made, b + 1)
                    dve.tensor_reduce(top[:, :], logits[:, :], AX.X, ALU.max).then_inc(top_found, 1)
                    wait(dve, top_found, b + 1)
                    dve.scalar_tensor_tensor(out=ranked[:, :], in0=logits[:, :], scalar=top[:, :],
                                             in1=rank[:, :], op0=ALU.is_ge,
                                             op1=ALU.mult).then_inc(ranked_made, 1)
                    wait(dve, ranked_made, b + 1)
                    dve.tensor_reduce(best[:, :], ranked[:, :], AX.X, ALU.max).then_inc(best_found, 1)
                    wait(dve, best_found, b + 1)
                    dve.tensor_scalar(neg_best[:, :], best[:, :], 1.0, -1.0, ALU.max,
                                      ALU.mult).then_inc(best_negated, 1)
                    wait(dve, best_negated, b + 1)
                    dve.tensor_scalar(expert_of[:, bass.ds(b, 1)], neg_best[:, :], float(E), None,
                                      ALU.add).then_inc(expert_known, 1)
                if live(t):
                    dve.tensor_reduce(abs_max[:, u % 2, :], prob[:, u % 2, :, :], AX.X, ALU.max,
                                      apply_absolute_value=True).then_inc(abs_found, 1)
                b = t + 1
                if live(b):
                    side, dpar = (u + 1) % 2, pv_mod(u, 1, 4) // 2
                    wait(dve, qk_rounded, b + 1)
                    dve.tensor_tensor(q_lo[:, :, :], qk[:, dpar, :, 0, side * P:side * P + P],
                                      q_hi[:, :, :].bitcast(F32), ALU.subtract)
                    for h in range(HPC):
                        last = dve.scalar_tensor_tensor(
                            out=k_lo[:, :, h, :], in0=qk[:, dpar, :, 1, side * P:side * P + P],
                            scalar=head_rows[:, h:h + 1], in1=k_hi[:, :, h, :].bitcast(F32),
                            op0=ALU.mult, op1=ALU.subtract)
                    last.then_inc(qk_split, 1)
                if isinstance(t, int) and -1 <= t <= E - 2:
                    split_expert(t + 1)
                b = t - 2
                if live(b):
                    p2 = u % 2
                    wait(dve, proj_done, b + 1)
                    wait(dve, ld_x[p2], 16 * (half(i, u, -2) + 1))
                    wait(dve, y_done, b - 1)
                    if not isinstance(t, int) or b // 2 > 0:
                        wait(dve, st_x1[p2], 16 * half(i, u, -2))
                    dve.tensor_tensor(x1[:, p2, :], ps_b[:, :], x_in[:, p2, :],
                                      ALU.add).then_inc(residual_added, 1)
                    wait(dve, residual_added, b + 1)
                    dve.bn_stats(stats[:, :], x1[:, p2, :]).then_inc(stats_taken, 1)
                b = t - 1
                if live(b):
                    wait(dve, oT_rounded, b + 1)
                    wait(dve, proj_done, b)
                    dve.tensor_tensor(oT_lo[:, :, :].rearrange("p c n -> p (c n)"), ps_c[:, :],
                                      oT_hi[:, :, :].rearrange("p c n -> p (c n)").bitcast(F32),
                                      ALU.subtract).then_inc(oT_split, 1)
                if live(t - 2):
                    wait(dve, stats_taken, t - 1)
                b = t - 3
                if live(b):
                    p4 = pv_mod(u, -3, 4)
                    wait(dve, ld_adjT[p4 // 2], 16 * (quarter(i, u, -3) + 1))
                    dve.tensor_reduce(adjT_in[:, p4 // 2, p4 % 2, P:P + 1], adjT_in[:, p4 // 2, p4 % 2, 0:P],
                                      AX.X, ALU.add).then_inc(rows_summed, 1)
                if live(t - 2):
                    dve.bn_aggr(mean_var[:, :], stats[:, :]).then_inc(stats_joined, 1)
                    b = t - 2
                    wait(dve, stats_joined, b + 1)
                    dve.tensor_scalar(var_eps[:, :], mean_var[:, 1:2], EPS, None,
                                      ALU.add).then_inc(var_ready, 1)
                b = t - 2
                if live(b):
                    wait(dve, rstd_made, b + 1)
                    dve.tensor_scalar(x1[:, u % 2, :], x1[:, u % 2, :], mean_var[:, 0:1], rstd[:, :],
                                      ALU.subtract, ALU.mult).then_inc(x1_ready, 1)

            run_slots(dve, slot, -2)

        phase_one.close()
        p1.close()
        phase_two(nc, ctx, locals())


def phase_two(nc, ctx, v):
    (B, D, E, C, N) = (v[k] for k in ("B", "D", "E", "C", "N"))
    out, x1_dram, conv_dram = v["out"], v["x1_dram"], v["conv_dram"]
    minus_half = v["minus_half"]
    ident = v["ident"]
    ones, expert_of = v["ones"], v["expert_of"]
    square_sum, conv_sum, bank = v["square_sum"], v["conv_sum"], v["bank"]
    G = 4
    NG = B // G
    RING = 8 if NG % 8 == 0 and NG > 8 else 4
    assert NG % RING == 0 and NG > RING

    def sb(name, shape, dt=F32):
        return ctx.enter_context(nc.sbuf_tensor(name, shape, dt))

    def sem(name):
        return ctx.enter_context(nc.semaphore(name))

    experts = sb("experts", [P, E * C * D])
    bn_scale = sb("bn_scale", [P, E * D])
    bn_shift = sb("bn_shift", [P, E * D])
    gamma_t = sb("gamma_t", [P, E, C])
    beta_t = sb("beta_t", [P, E, C])
    mean_t = sb("mean_t", [P, E, C])
    mean_sq_t = sb("mean_sq_t", [P, E, C])
    var_t = sb("var_t", [P, E, C])
    inv_std_t = sb("inv_std_t", [P, E, C])
    scale_t = sb("scale_t", [P, E, C])
    shift_t = sb("shift_t", [P, E, C])
    number = sb("number", [1, B])
    is_expert = sb("is_expert", [1, E, B])
    graphs = sb("graphs", [1, E])
    nodes = sb("nodes", [P, E])
    inv_nodes = sb("inv_nodes", [P, E])
    conv_in = sb("conv_in", [P, RING, G, D])
    x1_in = sb("x1_in", [P, RING, G, D])
    stats = sb("stats2", [P, G, 6])
    mean_var = sb("mean_var2", [P, 2, G, 2])
    var_eps = sb("var_eps2", [P, 2, G])
    rstd = sb("rstd2", [P, 2, G])
    shift = sb("shift2", [P, 2, G])

    ld_bn = sem("ld_bn")
    ld_experts = sem("ld_experts")
    ld_g = [sem(f"ld_g{i}") for i in range(RING)]
    st_g = [sem(f"st_g{i}") for i in range(RING)]
    summed = sem("summed")
    counted = sem("counted")
    var_known = sem("var_known")
    inverted = sem("inverted")
    table_step = sem("table_step")
    columns_ready = sem("columns_ready")
    spread = sem("spread")
    table_ready = sem("table_ready")
    dve_passed = sem("dve_passed")
    scaled = sem("scaled")
    shifted = sem("shifted")
    joined = sem("joined")
    stats_taken = sem("stats_taken2")
    stats_joined = sem("stats_joined2")
    var_ready = sem("var_ready2")
    rstd_made = sem("rstd_made2")
    shift_made = sem("shift_made2")
    finished = sem("finished")

    def run_groups(eng, group):
        for r in range(RING):
            group(0, r)
        with eng.Fori(1, NG // RING, 1) as k:
            for r in range(RING):
                group(k, r)

    block = ctx.enter_context(nc.Block())

    @block.sync
    def _(sp):
        sp.dma_start(experts[:, :], v["expert_w"]).then_inc(ld_experts, 16)
        sp.dma_start(gamma_t[:, :, :], v["gamma"]).then_inc(ld_bn, 16)
        sp.dma_start(beta_t[:, :, :], v["beta"]).then_inc(ld_bn, 16)

        def load(k, r):
            g = k * RING + r
            if not isinstance(k, int) or k > 0:
                sp.wait_ge(st_g[r], k * 16)
            sp.dma_start(conv_in[:, r, :, :], conv_dram[:, bass.ds(g * G, G), :]).then_inc(ld_g[r], 16)
            sp.dma_start(x1_in[:, r, :, :], x1_dram[:, bass.ds(g * G, G), :]).then_inc(ld_g[r], 16)

        run_groups(sp, load)

    @block.tensor
    def _(pe):
        for e in range(E):
            for j in range(C):
                pe.matmul(bank[0][:, e * C + j:e * C + j + 1],
                          square_sum[:, e * D + j * P:e * D + (j + 1) * P], ones[:, :], start=True, stop=True)
        pe.wait_ge(counted, 1)
        pe.matmul(bank[2][:, 0:E], ones[0:1, :].to_broadcast([1, P]), graphs[:, :], start=True, stop=True)
        pe.wait_ge(ld_experts, 16)
        for e in range(E):
            for j in range(C):
                for c in range(C):
                    row = (e * C + c) * D + j * P
                    last = pe.matmul(bank[1][:, e * C + j:e * C + j + 1], experts[:, row:row + P],
                                     conv_sum[:, e * C + c:e * C + c + 1], start=(c == 0), stop=(c == C - 1))
        last.then_inc(summed, 1)
        pe.wait_ge(columns_ready, 1)
        for table in range(2):
            for e in range(E):
                for j in range(C):
                    column = (scale_t, shift_t)[table][:, e, j:j + 1]
                    last = pe.matmul(bank[4 * table + e][:, j * P:(j + 1) * P],
                                     column.to_broadcast([P, P]), ident[:, :], start=True, stop=True)
                last.then_inc(spread, 1)

    @block.gpsimd
    def _(pool):
        pool.wait_ge(var_known, 1)
        pool.tensor_tensor(inv_std_t[:, :, :], var_t[:, :, :], minus_half[:, :].unsqueeze(2).to_broadcast(
            [P, E, C]), ALU.pow).then_inc(inverted, 1)
        pool.wait_ge(table_ready, 2 * E)

        def root(g, p2):
            pool.wait_ge(var_ready, g + 1)
            if not isinstance(g, int) or g > 1:
                pool.wait_ge(finished, g - 1)
            pool.tensor_tensor(rstd[:, p2, :], var_eps[:, p2, :], minus_half[:, :].to_broadcast([P, G]),
                               ALU.pow).then_inc(rstd_made, 1)

        def group(k, r):
            g = k * RING + r
            pool.wait_ge(ld_g[r], (k + 1) * 32)
            for j in range(G):
                e = pool.value_load(expert_of[0:1, bass.ds(g * G + j, 1)], min_val=0, max_val=E - 1)
                pool.tensor_tensor(conv_in[:, r, j, :], conv_in[:, r, j, :],
                                   bn_scale[:, bass.ds(e * D, D)], ALU.mult).then_inc(scaled, 1)
            if not isinstance(g, int) or g > 0:
                root(g - 1, (r - 1) % 2)

        run_groups(pool, group)
        root(NG - 1, (NG - 1) % 2)

    @block.scalar
    def _(act):
        for table in range(2):
            for e in range(E):
                act.wait_ge(spread, table * E + e + 1)
                act.activation((bn_scale, bn_shift)[table][:, e * D:(e + 1) * D], bank[4 * table + e][:, :],
                               ACT.Copy).then_inc(table_ready, 1)

        def group(k, r):
            g = k * RING + r
            act.wait_ge(shift_made, g + 1)
            for j in range(G):
                last = act.activation(x1_in[:, r, j, :], x1_in[:, r, j, :], ACT.Identity,
                                      bias=shift[:, r % 2, j:j + 1], scale=rstd[:, r % 2, j:j + 1])
            last.then_inc(finished, 1)
            act.wait_ge(finished, g + 1)
            act.dma_start(out[bass.ds(g * G, G), :, :].rearrange("b n d -> n b d"),
                          x1_in[:, r, :, :]).then_inc(st_g[r], 16)

        run_groups(act, group)
        for r in range(RING):
            act.wait_ge(st_g[r], 16 * (NG // RING))

    @block.vector
    def _(dve):
        steps = [0]

        def step(ins):
            steps[0] += 1
            ins.then_inc(table_step, 1)
            dve.wait_ge(table_step, steps[0])

        per_node = inv_nodes[:, :].unsqueeze(2).to_broadcast([P, E, C])
        step(dve.tensor_copy(number[:, :], expert_of[:, :]))
        for e in range(E):
            step(dve.tensor_scalar(is_expert[:, e, :], number[:, :], float(e), None, ALU.is_equal))
        dve.tensor_reduce(graphs[:, :], is_expert[:, :, :], AX.X, ALU.add).then_inc(counted, 1)
        dve.wait_ge(summed, 1)
        step(dve.tensor_scalar(nodes[:, :], bank[2][:, 0:E], float(N), 1.0, ALU.mult, ALU.max))
        step(dve.reciprocal(inv_nodes[:, :], nodes[:, :]))
        dve.wait_ge(ld_bn, 32)
        step(dve.tensor_tensor(mean_t[:, :, :], bank[1][:, 0:E * C].rearrange("p (e c) -> p e c", e=E),
                               per_node, ALU.mult))
        step(dve.tensor_tensor(mean_sq_t[:, :, :], mean_t[:, :, :], mean_t[:, :, :], ALU.mult))
        step(dve.tensor_tensor(var_t[:, :, :], bank[0][:, 0:E * C].rearrange("p (e c) -> p e c", e=E),
                               per_node, ALU.mult))
        step(dve.tensor_tensor(var_t[:, :, :], var_t[:, :, :], mean_sq_t[:, :, :], ALU.subtract))
        dve.tensor_scalar(var_t[:, :, :], var_t[:, :, :], EPS, None, ALU.add).then_inc(var_known, 1)
        dve.wait_ge(inverted, 1)
        step(dve.tensor_tensor(scale_t[:, :, :], gamma_t[:, :, :], inv_std_t[:, :, :], ALU.mult))
        step(dve.tensor_tensor(mean_t[:, :, :], mean_t[:, :, :], scale_t[:, :, :], ALU.mult))
        dve.tensor_tensor(shift_t[:, :, :], beta_t[:, :, :], mean_t[:, :, :],
                          ALU.subtract).then_inc(columns_ready, 1)
        dve.wait_ge(table_ready, 2 * E)

        def finish_stats(g, p2):
            dve.wait_ge(rstd_made, g + 1)
            if not isinstance(g, int) or g > 1:
                dve.wait_ge(finished, g - 1)
            dve.scalar_tensor_tensor(out=shift[:, p2, :], in0=mean_var[:, p2, :, 0], scalar=-1.0,
                                     in1=rstd[:, p2, :], op0=ALU.mult, op1=ALU.mult).then_inc(shift_made, 1)

        def group(k, r):
            g = k * RING + r
            for j in range(G):
                n = g * G + j
                e = dve.value_load(expert_of[0:1, bass.ds(n, 1)], min_val=0, max_val=E - 1)
                dve.wait_ge(scaled, n + 1)
                dve.tensor_tensor(conv_in[:, r, j, :], conv_in[:, r, j, :],
                                  bn_shift[:, bass.ds(e * D, D)], ALU.add).then_inc(shifted, 1)
            for j in range(G):
                dve.wait_ge(shifted, g * G + j + 1)
                dve.scalar_tensor_tensor(out=x1_in[:, r, j, :], in0=conv_in[:, r, j, :], scalar=0.0,
                                         in1=x1_in[:, r, j, :], op0=ALU.max,
                                         op1=ALU.add).then_inc(joined, 1)
            for j in range(G):
                dve.wait_ge(joined, g * G + j + 1)
                dve.bn_stats(stats[:, j, :], x1_in[:, r, j, :]).then_inc(stats_taken, 1)
            if not isinstance(g, int) or g > 0:
                finish_stats(g - 1, (r - 1) % 2)
            dve.wait_ge(stats_taken, (g + 1) * G)
            dve.sem_inc(dve_passed)
            for j in range(G):
                dve.bn_aggr(mean_var[:, r % 2, j, :], stats[:, j, :]).then_inc(stats_joined, 1)
            dve.wait_ge(stats_joined, (g + 1) * G)
            dve.tensor_scalar(var_eps[:, r % 2, :], mean_var[:, r % 2, :, 1], EPS, None,
                              ALU.add).then_inc(var_ready, 1)

        run_groups(dve, group)
        finish_stats(NG - 1, (NG - 1) % 2)


def kernel(x, adj, L0_gnn_Wq, L0_gnn_Wk, L0_gnn_Wv, L0_gnn_Wo, L1_gnn_router_w, L1_gnn_router_b,
           L1_gnn_expert_w, L1_gnn_bn_gamma, L1_gnn_bn_beta):
    import numpy as np
    import concourse.bacc as bacc
    from concourse.bass_utils import run_bass_kernel_spmd

    x, adj = np.asarray(x), np.asarray(adj)
    B, N, D = x.shape
    E = L1_gnn_bn_gamma.shape[0]
    C = D // P

    def weight(w):
        w = np.asarray(w).T.reshape(C, P, D)
        return w.transpose(1, 0, 2).reshape(P, C * D)

    arrays = {
        "x": x,
        "xT": x.reshape(B // 2, 2 * N, C, P).transpose(3, 0, 2, 1).reshape(P, B // 2, C * 2 * N),
        "adj": adj,
        "adjT": adj.transpose(2, 0, 1),
        "wqT": weight(L0_gnn_Wq), "wkT": weight(L0_gnn_Wk),
        "wvT": weight(L0_gnn_Wv), "woT": weight(L0_gnn_Wo),
        "router_w": np.asarray(L1_gnn_router_w).reshape(C, P, E).transpose(1, 0, 2),
        "router_b": np.asarray(L1_gnn_router_b),
        "expert_w": np.asarray(L1_gnn_expert_w).reshape(E, C, P, D).transpose(2, 0, 1, 3).reshape(P, E * C * D),
        "gamma": np.asarray(L1_gnn_bn_gamma).reshape(E, C, P).transpose(2, 0, 1),
        "beta": np.asarray(L1_gnn_bn_beta).reshape(E, C, P).transpose(2, 0, 1),
    }
    arrays = {k: np.ascontiguousarray(a) for k, a in arrays.items()}
    nc = bacc.Bacc("TRN2", target_bir_lowering=False, num_devices=1)
    ins = [nc.dram_tensor(k, a.shape, F32, kind="ExternalInput").ap() for k, a in arrays.items()]
    out = nc.dram_tensor("out", (B, N, D), F32, kind="ExternalOutput").ap()
    graph_block_program(nc, *ins, out)
    r = run_bass_kernel_spmd(nc, [arrays], core_ids=[0])
    return r.results[0]["out"]
```
